# Optimizing a Trainium2 kernel written in Bass

```python
import numpy as np
import jax
import jax.numpy as jnp

def _softmax(x, axis=-1):
    return jax.nn.softmax(x, axis=axis)

def _gelu(x):
    return jax.nn.gelu(x, approximate=True)

def _silu(x):
    return jax.nn.silu(x)

def _sigmoid(x):
    return jax.nn.sigmoid(x)

def _layernorm(x, axis=-1, eps=1e-05):
    m = jnp.mean(x, axis=axis, keepdims=True)
    v = jnp.var(x, axis=axis, keepdims=True)
    return (x - m) / jnp.sqrt(v + eps)

def _scatter_add(tgt, idx, src, axis=0):
    return tgt.at[idx].add(src)

def _segment_sum(src, seg, n):
    return jax.ops.segment_sum(src, seg, n)
kernel_name = 'mk_adj_preln_d1_adj_r2_8e7f77'

def setup_inputs(seed: int=0):
    np.random.seed(seed)
    _w = jnp.asarray

    def _rec_inputs():
        import jax
        import jax.numpy as jnp
        _gk = jax.random.key(seed)
        x = -0.0002928 + 1 * jax.random.normal(jax.random.fold_in(_gk, 1), (4096, 256), jnp.float32)
        _a = jax.random.bernoulli(jax.random.fold_in(_gk, 2), 0.000976562, (4096, 4096))
        _a = jnp.logical_or(_a, jnp.swapaxes(_a, -1, -2))
        _a = jnp.logical_or(_a, jnp.eye(4096, dtype=bool))
        _af = _a.astype(jnp.float32)
        adj = _af
        return (x, adj)
    x, adj = _rec_inputs()

    def _L0_gnn_setup():
        import jax, jax.numpy as jnp
        import numpy as np
        N = 4096
        D = 256
        L = 2
        NEG_SLOPE = 0.01

        def _gat_layer(x, W, adj):
            proj = x @ W
            Wh, Ws = jnp.split(proj, 2, axis=-1)
            scores = Wh @ Ws.T
            a = jax.nn.softmax(scores, axis=-1) * adj
            out = a @ Wh
            out = out + x
            return jax.nn.leaky_relu(out, NEG_SLOPE)
        key = jax.random.key(seed)
        k1, k2, k3 = jax.random.split(key, 3)
        inputs = jax.random.normal(k1, (N, D), dtype=jnp.float32)
        adj = jax.random.randint(k2, (N, N), 0, 2).astype(jnp.float32)
        W_stack = jax.random.normal(k3, (L, D, 2 * D), dtype=jnp.float32) * (1.0 / np.sqrt(D))
        return {'inputs': inputs, 'adj': adj, 'W_stack': W_stack}
    _L0_gnn_all = _L0_gnn_setup()
    _L0_gnn_in = {k: v for k, v in _L0_gnn_all.items() if k in ('W_stack',)}
    del _L0_gnn_all
    return {'x': x, 'adj': adj, 'L0_gnn_W_stack': _L0_gnn_in['W_stack']}

def reference(x, adj, L0_gnn_W_stack):
    import jax
    import jax.numpy as jnp

    def _L0_gnn_ref(inputs, adj, W_stack):
        import jax, jax.numpy as jnp
        import numpy as np
        N = 4096
        D = 256
        L = 2
        NEG_SLOPE = 0.01

        def _gat_layer(x, W, adj):
            proj = x @ W
            Wh, Ws = jnp.split(proj, 2, axis=-1)
            scores = Wh @ Ws.T
            a = jax.nn.softmax(scores, axis=-1) * adj
            out = a @ Wh
            out = out + x
            return jax.nn.leaky_relu(out, NEG_SLOPE)
        x = inputs
        for l in range(W_stack.shape[0]):
            x = _gat_layer(x, W_stack[l], adj)
        return x
    h = jnp.maximum(_layernorm(x, axis=-1), 0.0)
    x = x + _L0_gnn_ref(h, adj, L0_gnn_W_stack)
    return x

_drawn_inputs = setup_inputs


def setup_inputs(seed=0):
    import zlib

    import numpy as np

    out = dict(_drawn_inputs(seed))
    spreads = {}
    factors = {'adj': 4.039, 'L0_gnn_W_stack': 3.695}
    for name, (base, spread) in spreads.items():
        noise = np.random.default_rng([zlib.crc32(name.encode()), seed]).standard_normal(out[name].shape)
        drawn = base * np.exp(spread * noise) if base else spread * noise
        out[name] = jnp.asarray(drawn.astype(out[name].dtype))
    for name, factor in factors.items():
        out[name] = (out[name] * factor).astype(out[name].dtype)
    return out
```

```python
from contextlib import ExitStack

import concourse.bass as bass
from concourse import mybir

F32 = mybir.dt.float32
F32R = mybir.dt.float32r
ALU = mybir.AluOpType
ACT = mybir.ActivationFunctionType
AX = mybir.AxisListType

P = 128
HI, LO = 0, 1
EPS = 1e-5
SLOPE = 0.01
PRODUCTS = ((HI, HI), (HI, LO), (LO, HI))


def gnn_kernel(nc, x_padded, adj, w_value, w_transposed, out):
    N, D = out.shape
    LAYERS = w_value.shape[0]
    TILES = N // P
    CW = 512
    CHUNKS = N // CW
    STEPS = TILES * CHUNKS
    BLOCKS = CW // P
    KD = D // P
    ROUND = 2 * CHUNKS
    ROUNDS = STEPS // ROUND
    PAIRS = TILES // 2
    LAG_EXP = CHUNKS
    LAG_TRANSPOSE = CHUNKS + 2
    LAG_VALUE = LAG_TRANSPOSE + 1
    LAG_FINISH = LAG_VALUE + 1
    TAIL = LAG_FINISH
    LEAD = 4
    ADJ_SLOTS = 4

    adj_rows = adj.rearrange("(t p) n -> t p n", p=P)
    x_tiles = x_padded.rearrange("(t p) d -> t p d", p=P)
    out_tiles = out.rearrange("(t p) d -> t p d", p=P)
    feature_dram = nc.dram_tensor("feature_dram", [TILES, P, KD * 2 * P], F32, kind="Internal").ap()

    with ExitStack() as ctx:
        def sb(name, shape, dt=F32):
            return ctx.enter_context(nc.sbuf_tensor(name, shape, dt))

        def ps(name):
            return ctx.enter_context(nc.psum_tensor(name, [P, CW], F32))

        def sem(name):
            return ctx.enter_context(nc.semaphore(name))

        keys = sb("keys", [P, KD, 2, N], F32R)
        values = sb("values", [P, TILES, 2, D], F32R)
        scores = sb("scores", [P, ROUND, CW])
        adj_ring = sb("adj_ring", [P, ADJ_SLOTS, 2 * CW])
        split = sb("split", [P, 4, 2 * CW], F32R)
        query = sb("query", [P, 2, KD, 2, P], F32R)
        rows = sb("rows", [P, 2, 2, D])
        finished = sb("finished", [P, 2, D])
        residual = sb("residual", [P, D])
        addend = sb("addend", [P, D])
        low_part = sb("low_part", [P, D])
        ident = sb("ident", [P, P])
        chunk_max = sb("chunk_max", [P, 2, CHUNKS])
        neg_max = sb("neg_max", [P, 2])
        chunk_sum = sb("chunk_sum", [P, 2, CHUNKS])
        row_sum = sb("row_sum", [P, 1])
        inv_sum = sb("inv_sum", [P, 1])
        bn = sb("bn", [P, TILES, 6])
        mean = sb("mean", [P, TILES])
        rstd = sb("rstd", [P, TILES])
        var = sb("var", [P, TILES])
        tmp = sb("tmp", [P, TILES])
        x_all = scores[:, :, :].rearrange("p a (b d) -> p (a b) d", d=D)
        wt_raw = adj_ring[:, 0, :].rearrange("p (q d) -> p q d", d=D)
        wv_raw = adj_ring[:, 1, 0:KD * D].rearrange("p (q d) -> p q d", d=D)
        score_weight = split[:, 0, :].rearrange("p (e s d) -> p e s d", e=KD, s=2)
        value_weight = split[:, 1, :].rearrange("p (e s d) -> p e s d", e=KD, s=2)

        def pair_features(slot):
            return split[:, 2 + slot, :].rearrange("p (t e s r) -> p t e s r", t=2, e=KD, s=2)

        score_bank = [ps("score_bank0"), ps("score_bank1")]
        turn_bank = [ps("turn_bank0"), ps("turn_bank1")]
        sum_bank = [ps("sum_bank0"), ps("sum_bank1")]
        feature_bank = [ps("feature_bank0"), ps("feature_bank1")]

        ident_made = sem("ident_made")
        x_loaded = [sem(f"x_loaded{i}") for i in range(4)]
        stats_step = sem("stats_step")
        var_ready = sem("var_ready")
        sqrt_ready = sem("sqrt_ready")
        scaled = sem("scaled")
        weights_loaded = sem("weights_loaded")
        weight_product = sem("weight_product")
        weight_hi = sem("weight_hi")
        weight_lo = sem("weight_lo")
        rows_loaded = [sem("rows_loaded0"), sem("rows_loaded1")]
        rows_turned = sem("rows_turned")
        feature_hi = sem("feature_hi")
        feature_lo = sem("feature_lo")
        feature_stored = [sem("feature_stored0"), sem("feature_stored1")]
        key_product = sem("key_product")
        key_hi = sem("key_hi")
        key_lo = sem("key_lo")
        value_product = sem("value_product")
        value_hi = sem("value_hi")
        value_lo = sem("value_lo")
        adj_loaded = [sem(f"adj_loaded{i}") for i in range(ADJ_SLOTS)]
        query_loaded = [sem("query_loaded0"), sem("query_loaded1")]
        residual_loaded = sem("residual_loaded")
        scored = sem("scored")
        copied = sem("copied")
        maxed = sem("maxed")
        expd = sem("expd")
        masked = sem("masked")
        turned = sem("turned")
        split_hi = sem("split_hi")
        split_lo = sem("split_lo")
        summed = sem("summed")
        sum_ready = sem("sum_ready")
        inv_ready = sem("inv_ready")
        low_ready = sem("low_ready")
        finish_step = sem("finish_step")
        h_ready = sem("h_ready")
        h_stored = [sem("h_stored0"), sem("h_stored1")]

        def inside(k, c, lag):
            if isinstance(k, int):
                return 0 <= ROUND * k + c - lag < STEPS
            assert -ROUND <= c - lag < ROUND
            return True

        def done(layer, k, c, lag):
            return layer * STEPS + k * ROUND + (c - lag + 1)

        def later(k, c, lag, n):
            return not isinstance(k, int) or ROUND * k + c - lag >= n

        def tile(k, c):
            return k * 2 + c // CHUNKS

        def all_steps(eng, step):
            for c in range(ROUND):
                step(0, c)
            with eng.Fori(1, ROUNDS) as k:
                for c in range(ROUND):
                    step(k, c)
            for c in range(TAIL + LEAD):
                step(ROUNDS, c)

        def all_pairs(eng, step):
            for b in range(2):
                step(0, b)
            with eng.Fori(1, PAIRS // 2) as k:
                for b in range(2):
                    step(k, b)
            step(PAIRS // 2, 0)

        def after(k, b, lag, n):
            return not isinstance(k, int) or 2 * k + b - lag >= n

        def has_pair(k, b, lag):
            return not isinstance(k, int) or 0 <= 2 * k + b - lag < PAIRS

        block = ctx.enter_context(nc.Block())

        @block.sync
        def _(sp):
            n = TILES // 4
            for i in range(4):
                sp.dma_start(x_all[:, i * n:(i + 1) * n, :],
                             x_tiles[1 + i * n:1 + (i + 1) * n, :, :].rearrange("t p d -> p t d")
                             ).then_inc(x_loaded[i], 16)

            for i in range(4):
                sp.wait_ge(h_ready, (i + 1) * n)
                for b in range(2):
                    tiles = slice(i * n + b, (i + 1) * n, 2)
                    sp.dma_start(out_tiles[tiles, :, :].rearrange("t p d -> p t d"), x_all[:, tiles, :]
                                 ).then_inc(h_stored[b], 16 * n // 2)
            for b in range(2):
                sp.wait_ge(h_stored[b], 16 * PAIRS)

            with sp.Fori(0, LAYERS) as layer:
                sp.dma_start(wt_raw, w_transposed[bass.ds(layer, 1), :, :].rearrange(
                    "o (q p) d -> p (o q) d", p=P)).then_inc(weights_loaded, 16)
                sp.dma_start(wv_raw, w_value[bass.ds(layer, 1), :, :].rearrange(
                    "o (q p) d -> p (o q) d", p=P)).then_inc(weights_loaded, 16)

                def load_adj(k, c, lag):
                    u = (c - lag) % ROUND
                    slot = u // 2 % ADJ_SLOTS
                    cols = slice(u % CHUNKS * CW, (u % CHUNKS + 2) * CW)
                    sp.dma_start(adj_ring[:, slot, :],
                                 adj_rows[bass.ds(tile(k, c - lag), 1), :, cols].rearrange(
                                     "o p n -> p (o n)")).then_inc(adj_loaded[slot], 16)

                def load_query(k, c):
                    b = c // CHUNKS % 2
                    sp.dma_start(query[:, b, :, :, :].rearrange("p e s r -> p (e s r)").bitcast(F32),
                                 feature_dram[bass.ds(tile(k, c), 1), :, :].rearrange(
                                     "o p d -> p (o d)")).then_inc(query_loaded[b], 16)

                def pair(k, b):
                    if has_pair(k, b, 0):
                        for par in range(2):
                            sp.wait_ge(h_stored[par], layer * (16 * PAIRS) + k * 32 + 16 * (b + 1))
                        if after(k, b, 0, 2):
                            sp.wait_ge(rows_turned, layer * PAIRS + k * 2 + (b - 1))
                        sp.dma_start(rows[:, b, :, :], out_tiles[bass.ds(k * 4 + 2 * b, 2), :, :].rearrange(
                            "t p d -> p t d")).then_inc(rows_loaded[b], 16)
                    if has_pair(k, b, 1):
                        a = 1 - b
                        sp.wait_ge(feature_lo, layer * PAIRS + k * 2 + b)
                        sp.dma_start(feature_dram[bass.ds(k * 4 + 2 * (b - 1), 2), :, :].rearrange("t p f -> p t f"),
                                     split[:, 2 + a, :].bitcast(F32).rearrange("p (t f) -> p t f", t=2)
                                     ).then_inc(feature_stored[a], 16)

                pair(0, 0)
                pair(0, 1)
                sp.wait_ge(weight_lo, (layer + 1) * 2)
                for c in range(0, 2 * ADJ_SLOTS, 2):
                    load_adj(0, c, 0)
                with sp.Fori(1, PAIRS // 2) as k:
                    for b in range(2):
                        pair(k, b)
                pair(PAIRS // 2, 0)
                for b in range(2):
                    sp.wait_ge(feature_stored[b], (layer + 1) * (8 * PAIRS))
                load_query(0, 0)
                load_query(0, CHUNKS)

                def step(k, c):
                    if (c - LEAD) % 2 == 0 and inside(k, c, LEAD) and later(k, c, LEAD, 2 * ADJ_SLOTS):
                        sp.wait_ge(masked, done(layer, k, c, LEAD + 2 * ADJ_SLOTS - 1))
                        load_adj(k, c, LEAD)
                    if c % CHUNKS == 0 and inside(k, c, 0) and later(k, c, 0, 2 * CHUNKS):
                        sp.wait_ge(scored, done(layer, k, c, CHUNKS + 1))
                        load_query(k, c)
                    lag = LEAD + LAG_FINISH
                    if (c - lag) % CHUNKS == 0 and inside(k, c, lag):
                        t = tile(k, c - lag)
                        b = ((c - lag) // CHUNKS) % 2
                        tiles_before = (layer + 1) * TILES + t
                        sp.to_reg(tiles_before)
                        sp.wait_ge(h_stored[b], layer * (16 * PAIRS) + k * 16
                                   + 16 * ((c - lag) // ROUND + 1))
                        sp.wait_ge(h_ready, tiles_before)
                        sp.dma_start(residual[:, :], out_tiles[bass.ds(t, 1), :, :].rearrange(
                            "o p d -> p (o d)")).then_inc(residual_loaded, 16)
                        sp.dma_start(addend[:, :], x_tiles[bass.ds(layer * (t + 1), 1), :, :].rearrange(
                            "o p d -> p (o d)")).then_inc(residual_loaded, 16)
                    lag = LEAD + CHUNKS - 1 + LAG_FINISH
                    if (c - lag) % CHUNKS == 0 and inside(k, c, lag):
                        t = tile(k, c - lag)
                        b = (c - lag) // CHUNKS % 2
                        sp.wait_ge(h_ready, (layer + 1) * TILES + t + 1)
                        sp.dma_start(out_tiles[bass.ds(t, 1), :, :].rearrange("o p d -> p (o d)"),
                                     finished[:, b, :]).then_inc(h_stored[b], 16)

                all_steps(sp, step)

            for b in range(2):
                sp.wait_ge(h_stored[b], (LAYERS + 1) * PAIRS * 16)

        @block.tensor
        def _(pe):
            pe.wait_ge(ident_made, 2)
            with pe.Fori(0, LAYERS) as layer:
                pe.wait_ge(weights_loaded, (layer + 1) * 32)
                pe.wait_ge(h_ready, (layer + 1) * TILES - 1)
                for e in range(KD):
                    for q in range(KD):
                        last = nc.tensor.matmul(sum_bank[0][:, e * D:(e + 1) * D],
                                                wt_raw[:, KD + q, e * P:(e + 1) * P], wt_raw[:, q, :],
                                                start=(q == 0), stop=(q == KD - 1))
                last.then_inc(weight_product, 1)

                def pair(k, b):
                    if has_pair(k, b, 0):
                        pe.wait_ge(rows_loaded[b], layer * (8 * PAIRS) + k * 16 + 16)
                        for t in range(2):
                            for e in range(KD):
                                at = (t * KD + e) * P
                                last = nc.tensor.transpose(feature_bank[b][:, at:at + P],
                                                           rows[:, b, t, e * P:(e + 1) * P], ident[:, :])
                        last.then_inc(rows_turned, 1)
                    if not has_pair(k, b, 1):
                        return
                    a = 1 - b
                    h = pair_features(a)
                    pe.wait_ge(feature_lo, layer * PAIRS + k * 2 + b)
                    for d in range(KD):
                        for e in range(KD):
                            for i, (w, m) in enumerate(PRODUCTS):
                                last = nc.tensor.matmul(
                                    score_bank[a][:, d * 2 * P:(d + 1) * 2 * P],
                                    score_weight[:, e, w, d * P:(d + 1) * P], h[:, :, e, m, :],
                                    start=(e == 0 and i == 0), stop=(e == KD - 1 and i == 2))
                    last.then_inc(key_product, 1)
                    for t in range(2):
                        for e in range(KD):
                            for i, (w, m) in enumerate(PRODUCTS):
                                last = nc.tensor.matmul(
                                    turn_bank[a][:, t * D:(t + 1) * D],
                                    h[:, t, e, w, :], value_weight[:, e, m, :],
                                    start=(e == 0 and i == 0), stop=(e == KD - 1 and i == 2))
                    last.then_inc(value_product, 1)

                pe.wait_ge(weight_lo, (layer + 1) * 2)
                all_pairs(pe, pair)
                pe.wait_ge(key_lo, (layer + 1) * PAIRS)
                pe.wait_ge(value_lo, (layer + 1) * PAIRS)

                def score(k, c):
                    b = (c // CHUNKS) % 2
                    if c % CHUNKS == 0:
                        pe.wait_ge(query_loaded[b], layer * (16 * PAIRS) + k * 16 + 16)
                    if later(k, c, 0, 2):
                        pe.wait_ge(copied, done(layer, k, c, 2))
                    col = (c % CHUNKS) * CW
                    for e in range(KD):
                        for i, (a, m) in enumerate(PRODUCTS):
                            last = nc.tensor.matmul(score_bank[c % 2][:, :], query[:, b, e, a, :],
                                                    keys[:, e, m, col:col + CW],
                                                    start=(e == 0 and i == 0), stop=(e == KD - 1 and i == 2))
                    last.then_inc(scored, 1)

                def turn(k, c):
                    u = (c - LAG_TRANSPOSE) % ROUND
                    pe.wait_ge(masked, done(layer, k, c, LAG_TRANSPOSE))
                    if later(k, c, LAG_TRANSPOSE, 2):
                        pe.wait_ge(split_lo, done(layer, k, c, LAG_TRANSPOSE + 2))
                    for j in range(BLOCKS):
                        last = nc.tensor.transpose(turn_bank[u % 2][:, j * P:(j + 1) * P],
                                                   scores[:, u, j * P:(j + 1) * P], ident[:, :])
                    last.then_inc(turned, 1)

                def times_values(k, c):
                    u = (c - LAG_VALUE) % ROUND
                    t = u // CHUNKS
                    first, end = u % CHUNKS == 0, u % CHUNKS == CHUNKS - 1
                    pe.wait_ge(split_lo, done(layer, k, c, LAG_VALUE))
                    if first and later(k, c, LAG_VALUE, ROUND):
                        pe.wait_ge(h_ready, (layer + 1) * TILES + tile(k, c - LAG_VALUE) - 1)
                    for j in range(BLOCKS):
                        row = (u % CHUNKS) * BLOCKS + j
                        nc.tensor.matmul(sum_bank[t][:, :], split[:, u % 4, j * P:(j + 1) * P],
                                         values[:, row, :, :].rearrange("p s d -> p (s d)"),
                                         start=(first and j == 0), stop=False)
                        last = nc.tensor.matmul(sum_bank[t][:, 0:D],
                                                split[:, u % 4, CW + j * P:CW + (j + 1) * P],
                                                values[:, row, HI, :],
                                                start=False, stop=(end and j == BLOCKS - 1))
                    last.then_inc(summed, 1)

                def step(k, c):
                    if inside(k, c, 0):
                        score(k, c)
                    if inside(k, c, LAG_TRANSPOSE):
                        turn(k, c)
                    if inside(k, c, LAG_VALUE):
                        times_values(k, c)
                all_steps(pe, step)

        @block.vector
        def _(dve):
            n = [0]

            def link(instruction):
                n[0] += 1
                instruction.then_inc(stats_step, 1)
                dve.wait_ge(stats_step, n[0])

            for i in range(4):
                first, g = i * (TILES // 4), slice(i * (TILES // 4), (i + 1) * (TILES // 4))
                dve.wait_ge(x_loaded[i], 16)
                with dve.Fori(first, first + TILES // 4) as t:
                    nc.vector.bn_stats(bn[:, bass.ds(t, 1), :].rearrange("p o s -> p (o s)"),
                                       x_all[:, bass.ds(t, 1), :].rearrange("p o d -> p (o d)")
                                       ).then_inc(stats_step, 1)
                n[0] += TILES // 4
                dve.wait_ge(stats_step, n[0])
                link(nc.vector.tensor_tensor(mean[:, g], bn[:, g, 1], bn[:, g, 4], ALU.add))
                link(nc.vector.tensor_tensor(tmp[:, g], bn[:, g, 1], bn[:, g, 4], ALU.subtract))
                link(nc.vector.tensor_tensor(var[:, g], bn[:, g, 2], bn[:, g, 5], ALU.add))
                link(nc.vector.tensor_tensor(tmp[:, g], tmp[:, g], tmp[:, g], ALU.mult))
                link(nc.vector.tensor_scalar(mean[:, g], mean[:, g], 0.5, None, ALU.mult))
                link(nc.vector.tensor_scalar(var[:, g], var[:, g], 1.0 / D, EPS, ALU.mult, ALU.add))
                link(nc.vector.scalar_tensor_tensor(out=var[:, g], in0=tmp[:, g], scalar=0.25,
                                                    in1=var[:, g], op0=ALU.mult, op1=ALU.add))
                nc.vector.reciprocal(rstd[:, g], var[:, g]).then_inc(var_ready, 1)
                dve.wait_ge(sqrt_ready, i + 1)
                link(nc.vector.tensor_tensor(tmp[:, g], rstd[:, g], rstd[:, g], ALU.mult))
                link(nc.vector.tensor_tensor(tmp[:, g], tmp[:, g], var[:, g], ALU.mult))
                link(nc.vector.tensor_scalar(tmp[:, g], tmp[:, g], -0.5, 1.5, ALU.mult, ALU.add))
                link(nc.vector.tensor_tensor(rstd[:, g], rstd[:, g], tmp[:, g], ALU.mult))
                with dve.Fori(first, first + TILES // 4) as t:
                    row = x_all[:, bass.ds(t, 1), :].rearrange("p o d -> p (o d)")
                    nc.vector.tensor_scalar(row, row, mean[:, bass.ds(t, 1)], rstd[:, bass.ds(t, 1)],
                                            ALU.subtract, ALU.mult).then_inc(scaled, 1)

            with dve.Fori(0, LAYERS) as layer:
                dve.wait_ge(weight_hi, layer * 2 + 1)
                nc.vector.tensor_tensor(value_weight[:, :, LO, :], wv_raw,
                                        value_weight[:, :, HI, :].bitcast(F32),
                                        ALU.subtract).then_inc(weight_lo, 1)
                dve.wait_ge(weight_hi, layer * 2 + 2)
                nc.vector.tensor_tensor(score_weight[:, :, LO, :],
                                        sum_bank[0][:, :].rearrange("p (e d) -> p e d", e=KD),
                                        score_weight[:, :, HI, :].bitcast(F32),
                                        ALU.subtract).then_inc(weight_lo, 1)

                def pair(k, b):
                    if has_pair(k, b, 0):
                        h = split[:, 2 + b, :].rearrange("p (t s r) -> p t s r", t=2 * KD, s=2)
                        dve.wait_ge(feature_hi, layer * PAIRS + k * 2 + (b + 1))
                        nc.vector.tensor_tensor(h[:, :, LO, :],
                                                feature_bank[b][:, :].rearrange("p (t r) -> p t r", r=P),
                                                h[:, :, HI, :].bitcast(F32),
                                                ALU.subtract).then_inc(feature_lo, 1)
                    if has_pair(k, b, 1):
                        dve.wait_ge(key_hi, layer * PAIRS + k * 2 + b)
                        cols = bass.ds((k * 2 + (b - 1)) * (2 * P), 2 * P)
                        nc.vector.tensor_tensor(keys[:, :, LO, cols],
                                                score_bank[1 - b][:, :].rearrange("p (d r) -> p d r", d=KD),
                                                keys[:, :, HI, cols].bitcast(F32),
                                                ALU.subtract).then_inc(key_lo, 1)
                        dve.wait_ge(value_hi, layer * PAIRS + k * 2 + b)
                        at = bass.ds((k * 2 + (b - 1)) * 2, 2)
                        nc.vector.tensor_tensor(values[:, at, LO, :],
                                                turn_bank[1 - b][:, :].rearrange("p (t d) -> p t d", t=2),
                                                values[:, at, HI, :].bitcast(F32),
                                                ALU.subtract).then_inc(value_lo, 1)

                all_pairs(dve, pair)

                def copy(k, c):
                    t = (c // CHUNKS) % 2
                    dve.wait_ge(scored, done(layer, k, c, 0))
                    nc.vector.tensor_scalar(scores[:, c, :], score_bank[c % 2][:, :], 1.0, None, ALU.mult,
                                            ALU.max, accum_out=chunk_max[:, t, c % CHUNKS:c % CHUNKS + 1]
                                            ).then_inc(copied, 1)
                    if c % CHUNKS == CHUNKS - 1:
                        dve.wait_ge(copied, done(layer, k, c, 0))
                        nc.vector.tensor_reduce(neg_max[:, t:t + 1], chunk_max[:, t, :], AX.X, ALU.max,
                                                negate=True).then_inc(maxed, 1)

                def split_turned(k, c):
                    u = (c - LAG_TRANSPOSE) % ROUND
                    dve.wait_ge(split_hi, done(layer, k, c, LAG_TRANSPOSE))
                    nc.vector.tensor_tensor(split[:, u % 4, CW:2 * CW], turn_bank[u % 2][:, :],
                                            split[:, u % 4, 0:CW].bitcast(F32),
                                            ALU.subtract).then_inc(split_lo, 1)

                def invert_sum(k, c, lag):
                    b = ((c - lag) // CHUNKS) % 2
                    T = layer * TILES + tile(k, c - lag)
                    dve.wait_ge(expd, done(layer, k, c, lag - CHUNKS + 1))
                    nc.vector.tensor_reduce(row_sum[:, :], chunk_sum[:, b, :], AX.X, ALU.add
                                            ).then_inc(sum_ready, 1)
                    dve.wait_ge(sum_ready, T + 1)
                    nc.vector.reciprocal(inv_sum[:, :], row_sum[:, :]).then_inc(inv_ready, 1)

                def finish(k, c, lag):
                    b = ((c - lag) // CHUNKS) % 2
                    t = tile(k, c - lag)
                    T = layer * TILES + t
                    dve.wait_ge(low_ready, T + 1)
                    dve.wait_ge(h_stored[b], (layer + 1) * (16 * PAIRS) + k * 16 + 16 * ((c - lag) // ROUND))
                    nc.vector.scalar_tensor_tensor(out=finished[:, b, :], in0=sum_bank[b][:, 0:D],
                                                   scalar=inv_sum[:, :], in1=low_part[:, :],
                                                   op0=ALU.mult, op1=ALU.add).then_inc(finish_step, 1)
                    dve.wait_ge(residual_loaded, (T + 1) * 32)
                    dve.wait_ge(finish_step, T * 3 + 1)
                    nc.vector.tensor_tensor(finished[:, b, :], finished[:, b, :], residual[:, :],
                                            ALU.add).then_inc(finish_step, 1)
                    dve.wait_ge(finish_step, T * 3 + 2)
                    nc.vector.scalar_tensor_tensor(out=finished[:, b, :], in0=finished[:, b, :],
                                                   scalar=SLOPE, in1=finished[:, b, :],
                                                   op0=ALU.mult, op1=ALU.max).then_inc(finish_step, 1)
                    dve.wait_ge(finish_step, T * 3 + 3)
                    nc.vector.tensor_tensor(finished[:, b, :], finished[:, b, :], addend[:, :],
                                            ALU.add).then_inc(h_ready, 1)

                def step(k, c):
                    if inside(k, c, 0):
                        copy(k, c)
                    if inside(k, c, LAG_TRANSPOSE):
                        split_turned(k, c)
                    lag = CHUNKS - 1 + LAG_FINISH
                    if (c + 1 - lag) % CHUNKS == 0 and inside(k, c + 1, lag):
                        invert_sum(k, c + 1, lag)
                    if (c - lag) % CHUNKS == 0 and inside(k, c, lag):
                        finish(k, c, lag)
                all_steps(dve, step)

        @block.scalar
        def _(act):
            for i in range(4):
                first, g = i * (TILES // 4), slice(i * (TILES // 4), (i + 1) * (TILES // 4))
                act.wait_ge(var_ready, i + 1)
                nc.scalar.activation(rstd[:, g], rstd[:, g], ACT.Sqrt).then_inc(sqrt_ready, 1)
                act.wait_ge(scaled, first + TILES // 4)
                nc.scalar.activation(x_all[:, g, :], x_all[:, g, :], ACT.Relu
                                     ).then_inc(h_ready, TILES // 4)
            nc.scalar.preload_act_table(ACT.Exp)

            with act.Fori(0, LAYERS) as layer:
                act.wait_ge(weight_product, layer + 1)
                nc.scalar.activation(value_weight[:, :, HI, :], wv_raw, ACT.Copy).then_inc(weight_hi, 1)
                nc.scalar.activation(score_weight[:, :, HI, :],
                                     sum_bank[0][:, :].rearrange("p (e d) -> p e d", e=KD),
                                     ACT.Copy).then_inc(weight_hi, 1)

                def pair(k, b):
                    if has_pair(k, b, 0):
                        h = split[:, 2 + b, :].rearrange("p (t s r) -> p t s r", t=2 * KD, s=2)
                        act.wait_ge(rows_turned, layer * PAIRS + k * 2 + (b + 1))
                        if after(k, b, 0, 2):
                            act.wait_ge(feature_stored[b], layer * (8 * PAIRS) + k * 16)
                        nc.scalar.activation(h[:, :, HI, :],
                                             feature_bank[b][:, :].rearrange("p (t r) -> p t r", r=P),
                                             ACT.Copy).then_inc(feature_hi, 1)
                    if has_pair(k, b, 1):
                        act.wait_ge(key_product, layer * PAIRS + k * 2 + b)
                        nc.scalar.activation(keys[:, :, HI, bass.ds((k * 2 + (b - 1)) * (2 * P), 2 * P)],
                                             score_bank[1 - b][:, :].rearrange("p (d r) -> p d r", d=KD),
                                             ACT.Copy).then_inc(key_hi, 1)
                        act.wait_ge(value_product, layer * PAIRS + k * 2 + b)
                        nc.scalar.activation(values[:, bass.ds((k * 2 + (b - 1)) * 2, 2), HI, :],
                                             turn_bank[1 - b][:, :].rearrange("p (t d) -> p t d", t=2),
                                             ACT.Copy).then_inc(value_hi, 1)

                all_pairs(act, pair)
                for b in range(2):
                    act.wait_ge(feature_stored[b], (layer + 1) * (8 * PAIRS))

                def exponentials(k, c):
                    u = (c - LAG_EXP) % ROUND
                    t = u // CHUNKS
                    if u % CHUNKS == 0:
                        act.wait_ge(maxed, layer * TILES + tile(k, c - LAG_EXP) + 1)
                    nc.scalar.activation(scores[:, u, :], scores[:, u, :], ACT.Exp, bias=neg_max[:, t:t + 1],
                                         accum_out=chunk_sum[:, t, u % CHUNKS:u % CHUNKS + 1]
                                         ).then_inc(expd, 1)

                def split_turned(k, c):
                    u = (c - LAG_TRANSPOSE) % ROUND
                    act.wait_ge(turned, done(layer, k, c, LAG_TRANSPOSE))
                    if later(k, c, LAG_TRANSPOSE, 4):
                        act.wait_ge(summed, done(layer, k, c, LAG_TRANSPOSE + 4))
                    nc.scalar.activation(split[:, u % 4, 0:CW], turn_bank[u % 2][:, :], ACT.Copy
                                         ).then_inc(split_hi, 1)

                def scale_low(k, c, lag):
                    b = ((c - lag) // CHUNKS) % 2
                    T = layer * TILES + tile(k, c - lag)
                    act.wait_ge(summed, done(layer, k, c, LAG_FINISH))
                    act.wait_ge(inv_ready, T + 1)
                    nc.scalar.activation(low_part[:, :], sum_bank[b][:, D:2 * D], ACT.Copy,
                                         scale=inv_sum[:, :]).then_inc(low_ready, 1)

                def step(k, c):
                    if inside(k, c, LAG_EXP):
                        exponentials(k, c)
                    if inside(k, c, LAG_TRANSPOSE):
                        split_turned(k, c)
                    lag = CHUNKS - 1 + LAG_FINISH
                    if (c - lag) % CHUNKS == 0 and inside(k, c, lag):
                        scale_low(k, c, lag)
                all_steps(act, step)

        @block.gpsimd
        def _(pool):
            nc.gpsimd.memset(ident[:, :], 0.0).then_inc(ident_made, 1)
            pool.wait_ge(ident_made, 1)
            nc.gpsimd.affine_select(out=ident[:, :], in_=ident[:, :], compare_op=ALU.not_equal, fill=1.0,
                                    base=0, pattern=[[-1, P]], channel_multiplier=1).then_inc(ident_made, 1)

            with pool.Fori(0, LAYERS) as layer:
                def step(k, c):
                    if not inside(k, c, LAG_EXP):
                        return
                    u = (c - LAG_EXP) % ROUND
                    slot = (u // 2) % ADJ_SLOTS
                    pool.wait_ge(expd, done(layer, k, c, LAG_EXP))
                    if u % 2 == 0:
                        pool.wait_ge(adj_loaded[slot], layer * (32 * ROUNDS) + k * 32
                                     + 16 * ((c - LAG_EXP) // (2 * ADJ_SLOTS) + 1))
                    half = (u % 2) * CW
                    nc.gpsimd.tensor_tensor(scores[:, u, :], scores[:, u, :],
                                            adj_ring[:, slot, half:half + CW], ALU.mult).then_inc(masked, 1)

                all_steps(pool, step)


def kernel(x, adj, L0_gnn_W_stack):
    import numpy as np
    import concourse.bacc as bacc
    from concourse.bass_utils import run_bass_kernel_spmd

    x, adj, w = (np.asarray(a) for a in (x, adj, L0_gnn_W_stack))
    d = x.shape[1]
    arrays = {
        "x_padded": np.ascontiguousarray(np.concatenate([np.zeros((P, d), x.dtype), x])),
        "adj": np.ascontiguousarray(adj),
        "w_value": np.ascontiguousarray(w[:, :, 0:d]),
        "w_transposed": np.ascontiguousarray(w.transpose(0, 2, 1)),
    }
    nc = bacc.Bacc("TRN2", target_bir_lowering=False, num_devices=1)
    ins = [nc.dram_tensor(n, a.shape, mybir.dt.from_np(a.dtype), kind="ExternalInput").ap()
           for n, a in arrays.items()]
    out = nc.dram_tensor("out", x.shape, mybir.dt.from_np(x.dtype), kind="ExternalOutput").ap()
    gnn_kernel(nc, *ins, out)
    result = run_bass_kernel_spmd(nc, [arrays], core_ids=[0])
    return result.results[0]["out"]
```

```python
from contextlib import ExitStack

import concourse.bass as bass
from concourse import mybir

F32 = mybir.dt.float32
F32R = mybir.dt.float32r
ALU = mybir.AluOpType
ACT = mybir.ActivationFunctionType
AX = mybir.AxisListType

P = 128
HI, LO = 0, 1
EPS = 1e-5
SLOPE = 0.01
PRODUCTS = ((HI, HI), (HI, LO), (LO, HI))


def gnn_kernel(nc, x_padded, adj, w_value, w_transposed, out):
    N, D = out.shape
    LAYERS = w_value.shape[0]
    TILES = N // P
    CW = 512
    CHUNKS = N // CW
    STEPS = TILES * CHUNKS
    BLOCKS = CW // P
    KD = D // P
    ROUND = 2 * CHUNKS
    ROUNDS = STEPS // ROUND
    PAIRS = TILES // 2
    Q = 32
    RUNS = P // Q
    GROUP = 2 * CW
    RUN = GROUP // RUNS
    PAIR_ROUND = GROUP // (2 * P)
    LAG_EXP = CHUNKS
    LAG_TURN = CHUNKS + 1
    LAG_SHUFFLE = CHUNKS + 3
    LAG_SPLIT = CHUNKS + 5
    LAG_VALUE = LAG_SPLIT + 1
    LAG_FINISH = LAG_VALUE + 1
    TAIL = ROUND
    LEAD = 4
    ADJ_SLOTS = 4

    assert GROUP // P * RUNS * Q == GROUP and CHUNKS % 2 == 0 and PAIRS % PAIR_ROUND == 0
    adj_rows = adj.rearrange("(t p) n -> t p n", p=P)
    x_tiles = x_padded.rearrange("(t p) d -> t p d", p=P)
    out_tiles = out.rearrange("(t p) d -> t p d", p=P)
    feature_dram = nc.dram_tensor("feature_dram", [TILES, P, KD * 2 * P], F32, kind="Internal").ap()
    weight_dram = nc.dram_tensor("weight_dram", [LAYERS, 2, P, KD * 2 * D], F32, kind="Internal").ap()

    with ExitStack() as ctx:
        def sb(name, shape, dt=F32):
            return ctx.enter_context(nc.sbuf_tensor(name, shape, dt))

        def ps(name):
            return ctx.enter_context(nc.psum_tensor(name, [P, CW], F32))

        def sem(name):
            return ctx.enter_context(nc.semaphore(name))

        keys = sb("keys", [P, KD, 2, N], F32R)
        turned_ring = sb("turned_ring", [P, 2, RUNS, RUN], F32R)
        values = sb("values", [P, TILES, 2, D], F32R)
        scores = sb("scores", [P, ROUND, CW])
        adj_ring = sb("adj_ring", [P, ADJ_SLOTS, 2 * CW])
        split = sb("split", [P, 4, 2 * CW], F32R)
        query = sb("query", [P, 2, KD, 2, P], F32R)
        rows = sb("rows", [P, PAIR_ROUND, 2, D])
        finished = sb("finished", [P, 2, D])
        residual = sb("residual", [P, D])
        addend = sb("addend", [P, D])
        low_part = sb("low_part", [P, D])
        ident = sb("ident", [P, P])
        chunk_max = sb("chunk_max", [P, 2, CHUNKS])
        neg_max = sb("neg_max", [P, 2])
        chunk_sum = sb("chunk_sum", [P, 2, CHUNKS])
        row_sum = sb("row_sum", [P, 1])
        inv_sum = sb("inv_sum", [P, 1])
        bn = sb("bn", [P, TILES, 6])
        mean = sb("mean", [P, TILES])
        rstd = sb("rstd", [P, TILES])
        var = sb("var", [P, TILES])
        tmp = sb("tmp", [P, TILES])
        shift = sb("shift", [P, TILES])
        x_all = scores[:, :, :].rearrange("p a (b d) -> p (a b) d", d=D)
        wt_raw = [adj_ring[:, 2 * l, :].rearrange("p (q d) -> p q d", d=D) for l in range(LAYERS)]
        wv_raw = [adj_ring[:, 2 * l + 1, 0:KD * D].rearrange("p (q d) -> p q d", d=D) for l in range(LAYERS)]

        score_weights = [split[:, l, :].rearrange("p (e s d) -> p e s d", e=KD, s=2) for l in range(LAYERS)]
        value_weights = [turned_ring[:, l, :, :].rearrange("p a (s d) -> p (a s) d", d=D).rearrange(
            "p (e s) d -> p e s d", e=KD) for l in range(LAYERS)]
        score_weight, value_weight = score_weights[0], value_weights[0]

        keys_by_run = keys[:, :, :, :].rearrange("p d s (g b x) -> p d s g b x", b=RUNS, x=RUN)

        def pair_keys(part, k, b):
            u = b % PAIR_ROUND
            return keys_by_run[:, :, part, bass.ds(k + b // PAIR_ROUND, 1), :, 2 * Q * u:2 * Q * (u + 1)
                               ].rearrange("p d o b x -> p d (o b) x")

        def turned_chunk(u):
            return turned_ring[:, u // 2 % 2, :, u % 2 * (RUN // 2):(u % 2 + 1) * (RUN // 2)].bitcast(F32).rearrange(
                "p a (j i) -> p j a i", i=Q)

        def by_run(bank):
            return bank[:, :].rearrange("p (d x b) -> p d b x", d=KD, b=RUNS)

        def pair_features(slot):
            return split[:, 2 + slot, :].rearrange("p (t e s r) -> p t e s r", t=2, e=KD, s=2)

        score_bank = [ps(f"score_bank{i}") for i in range(4)]
        value_bank = score_bank[2:4]
        sum_bank = [ps("sum_bank0"), ps("sum_bank1")]
        feature_bank = [ps("feature_bank0"), ps("feature_bank1")]

        ident_made = sem("ident_made")
        x_loaded = [sem(f"x_loaded{i}") for i in range(4)]
        stats_step = sem("stats_step")
        var_ready = sem("var_ready")
        sqrt_ready = sem("sqrt_ready")
        scale_ready = sem("scale_ready")
        weights_loaded = sem("weights_loaded")
        weight_product = sem("weight_product")
        weight_hi = sem("weight_hi")
        weight_lo = sem("weight_lo")
        weights_stored = sem("weights_stored")
        weights_ready = sem("weights_ready")
        rows_loaded = [sem(f"rows_loaded{i}") for i in range(PAIR_ROUND)]
        rows_turned = sem("rows_turned")
        feature_hi = sem("feature_hi")
        feature_lo = sem("feature_lo")
        feature_stored = [sem("feature_stored0"), sem("feature_stored1")]
        key_product = sem("key_product")
        key_hi = sem("key_hi")
        key_lo = sem("key_lo")
        value_product = sem("value_product")
        value_hi = sem("value_hi")
        value_lo = sem("value_lo")
        adj_loaded = [sem(f"adj_loaded{i}") for i in range(ADJ_SLOTS)]
        query_loaded = [sem("query_loaded0"), sem("query_loaded1")]
        residual_loaded = sem("residual_loaded")
        scored = sem("scored")
        copied = sem("copied")
        maxed = sem("maxed")
        expd = sem("expd")
        masked = sem("masked")
        turned = sem("turned")
        shuffled = [sem("shuffled0"), sem("shuffled1")]
        split_hi = sem("split_hi")
        split_lo = sem("split_lo")
        summed = sem("summed")
        sum_ready = sem("sum_ready")
        inv_ready = sem("inv_ready")
        low_ready = sem("low_ready")
        finish_step = sem("finish_step")
        h_ready = sem("h_ready")
        h_stored = [sem("h_stored0"), sem("h_stored1")]

        def inside(k, c, lag):
            if isinstance(k, int):
                return 0 <= ROUND * k + c - lag < STEPS
            assert -ROUND <= c - lag < ROUND
            return True

        def done(layer, k, c, lag):
            return layer * STEPS + k * ROUND + (c - lag + 1)

        def later(k, c, lag, n):
            return not isinstance(k, int) or ROUND * k + c - lag >= n

        def tile(k, c):
            return k * 2 + c // CHUNKS

        def all_steps(eng, step):
            for c in range(ROUND):
                step(0, c)
            with eng.Fori(1, ROUNDS) as k:
                for c in range(ROUND):
                    step(k, c)
            for c in range(TAIL):
                step(ROUNDS, c)

        def all_pairs(eng, step, lag):
            for b in range(PAIR_ROUND):
                step(0, b)
            with eng.Fori(1, PAIRS // PAIR_ROUND) as k:
                for b in range(PAIR_ROUND):
                    step(k, b)
            for b in range(lag):
                step(PAIRS // PAIR_ROUND, b)

        def after(k, b, lag, n):
            return not isinstance(k, int) or PAIR_ROUND * k + b - lag >= n

        def has_pair(k, b, lag):
            return not isinstance(k, int) or 0 <= PAIR_ROUND * k + b - lag < PAIRS

        def pairs_done(layer, k, b, lag):
            return layer * PAIRS + k * PAIR_ROUND + (b - lag + 1)

        def shuffles_done(layer, k, u):
            return layer * (STEPS // 4 * 64) + k * (ROUND // 4 * 64) + 64 * (u // 4 + 1)

        block = ctx.enter_context(nc.Block())

        @block.sync
        def _(sp):
            n = TILES // 4

            def load_x(i):
                sp.dma_start(x_all[:, i * n:(i + 1) * n, :],
                             x_tiles[1 + i * n:1 + (i + 1) * n, :, :].rearrange("t p d -> p t d")
                             ).then_inc(x_loaded[i], 16)

            load_x(0)
            for l in range(LAYERS):
                sp.dma_start(wt_raw[l], w_transposed[l, :, :].rearrange("(q p) d -> p q d", p=P)
                             ).then_inc(weights_loaded, 16)
                sp.dma_start(wv_raw[l], w_value[l, :, :].rearrange("(q p) d -> p q d", p=P)
                             ).then_inc(weights_loaded, 16)
            for i in range(1, 4):
                load_x(i)

            def load_rows(b, first_tile):
                sp.dma_start(rows[:, b, :, :], out_tiles[bass.ds(first_tile, 2), :, :].rearrange(
                    "t p d -> p t d")).then_inc(rows_loaded[b], 16)

            for i in range(4):
                sp.wait_ge(h_ready, (i + 1) * n)
                for b in range(2):
                    tiles = slice(i * n + b, (i + 1) * n, 2)
                    sp.dma_start(out_tiles[tiles, :, :].rearrange("t p d -> p t d"), x_all[:, tiles, :]
                                 ).then_inc(h_stored[b], 16 * n // 2)
                for b in range(2):
                    sp.wait_ge(h_stored[b], (i + 1) * (16 * n // 2))
                if i == 0:
                    for b in range(PAIR_ROUND):
                        load_rows(b, 2 * b)

            with sp.Fori(0, LAYERS) as layer:
                def load_adj(k, c, lag):
                    u = (c - lag) % ROUND
                    slot = u // 2 % ADJ_SLOTS
                    cols = slice(u % CHUNKS * CW, (u % CHUNKS + 2) * CW)
                    sp.dma_start(adj_ring[:, slot, :],
                                 adj_rows[bass.ds(tile(k, c - lag), 1), :, cols].rearrange(
                                     "o p n -> p (o n)")).then_inc(adj_loaded[slot], 16)

                def load_query(k, c):
                    b = c // CHUNKS % 2
                    sp.dma_start(query[:, b, :, :, :].rearrange("p e s r -> p (e s r)").bitcast(F32),
                                 feature_dram[bass.ds(tile(k, c), 1), :, :].rearrange(
                                     "o p d -> p (o d)")).then_inc(query_loaded[b], 16)

                def pair(k, b):
                    if has_pair(k, b, 0) and after(k, b, 0, PAIR_ROUND):
                        pair_before = pairs_done(layer, k, b, PAIR_ROUND)
                        sp.to_reg(pair_before)
                        for par in range(2):
                            sp.wait_ge(h_stored[par], layer * (16 * PAIRS) + k * (16 * PAIR_ROUND) + 16 * (b + 1))
                        sp.wait_ge(rows_turned, pair_before)
                        load_rows(b, k * (2 * PAIR_ROUND) + 2 * b)
                    if has_pair(k, b, 2):
                        sp.wait_ge(feature_lo, pairs_done(layer, k, b, 2))
                        sp.dma_start(feature_dram[bass.ds(k * (2 * PAIR_ROUND) + 2 * (b - 2), 2), :, :
                                                  ].rearrange("t p f -> p t f"),
                                     split[:, 2 + b % 2, :].bitcast(F32).rearrange("p (t f) -> p t f", t=2)
                                     ).then_inc(feature_stored[b % 2], 16)

                for b in range(PAIR_ROUND):
                    pair(0, b)
                with sp.Fori(1, PAIRS // PAIR_ROUND) as k:
                    for b in range(PAIR_ROUND):
                        pair(k, b)
                sp.wait_ge(feature_stored[0], layer * (8 * PAIRS) + 16)
                load_query(0, 0)
                load_query(0, CHUNKS)
                for b in range(2):
                    pair(PAIRS // PAIR_ROUND, b)
                for b in range(2):
                    sp.wait_ge(feature_stored[b], (layer + 1) * (8 * PAIRS))
                sp.wait_ge(weights_stored, LAYERS * 32)
                for c in range(0, 2 * ADJ_SLOTS, 2):
                    load_adj(0, c, 0)

                def next_layer():
                    for b in range(2):
                        sp.wait_ge(h_stored[b], (layer + 1) * (16 * PAIRS) + 16 * PAIR_ROUND)
                    for b in range(PAIR_ROUND):
                        load_rows(b, 2 * b)
                    sp.wait_ge(summed, (layer + 1) * STEPS - 2)
                    for which, target in enumerate((
                            split[:, 0, :], turned_ring[:, 0, :, :].rearrange("p a x -> p (a x)"))):
                        sp.dma_start(target.bitcast(F32), weight_dram[bass.ds(layer, 1), which, :, :].rearrange(
                            "o p w -> p (o w)")).then_inc(weights_ready, 16)

                def step(k, c):
                    if (c - LEAD) % 2 == 0 and inside(k, c, LEAD) and later(k, c, LEAD, 2 * ADJ_SLOTS):
                        sp.wait_ge(masked, done(layer, k, c, LEAD + 2 * ADJ_SLOTS - 1))
                        load_adj(k, c, LEAD)
                    if c % CHUNKS == 0 and inside(k, c, 0) and later(k, c, 0, 2 * CHUNKS):
                        sp.wait_ge(scored, done(layer, k, c, CHUNKS + 1))
                        load_query(k, c)
                    if inside(k, c, LAG_SHUFFLE + 1) and (c - LAG_SHUFFLE - 1) % 2 == 1:
                        u = (c - LAG_SHUFFLE - 1) % ROUND
                        slot = u // 2 % 2
                        group_before = done(layer, k, c, LAG_SHUFFLE + 5)
                        if later(k, c, LAG_SHUFFLE + 1, 4):
                            sp.to_reg(group_before)
                        sp.wait_ge(turned, done(layer, k, c, LAG_SHUFFLE + 1))
                        if later(k, c, LAG_SHUFFLE + 1, 4):
                            sp.wait_ge(split_lo, group_before)
                        for a in range(RUNS):
                            sp.dma_start(turned_ring[:, slot, a, :].bitcast(F32),
                                         scores[a * Q:(a + 1) * Q, u - 1:u + 1, :]
                                         ).then_inc(shuffled[slot], 16)
                    lag = LEAD + LAG_FINISH - 2
                    if (c - lag) % CHUNKS == 0 and inside(k, c, lag):
                        t = tile(k, c - lag)
                        b = ((c - lag) // CHUNKS) % 2
                        tiles_before = (layer + 1) * TILES + t
                        sp.to_reg(tiles_before)
                        sp.wait_ge(h_stored[b], layer * (16 * PAIRS) + k * 16
                                   + 16 * ((c - lag) // ROUND + 1))
                        sp.wait_ge(h_ready, tiles_before)
                        sp.dma_start(residual[:, :], out_tiles[bass.ds(t, 1), :, :].rearrange(
                            "o p d -> p (o d)")).then_inc(residual_loaded, 16)
                        sp.dma_start(addend[:, :], x_tiles[bass.ds(layer * (t + 1), 1), :, :].rearrange(
                            "o p d -> p (o d)")).then_inc(residual_loaded, 16)

                all_steps(sp, step)
                next_layer()

            for b in range(2):
                sp.wait_ge(h_stored[b], (LAYERS + 1) * PAIRS * 16)
            for b in range(PAIR_ROUND):
                sp.wait_ge(rows_loaded[b], (LAYERS * PAIRS // PAIR_ROUND + 1) * 16)
            sp.wait_ge(weights_ready, (LAYERS + 1) * 32)
            sp.wait_ge(weights_stored, LAYERS * 32)

        @block.tensor
        def _(pe):
            pe.wait_ge(ident_made, 2)
            pe.wait_ge(weights_loaded, LAYERS * 32)
            for l in range(LAYERS):
                for e in range(KD):
                    for q in range(KD):
                        last = nc.tensor.matmul(sum_bank[l][:, e * D:(e + 1) * D],
                                                wt_raw[l][:, KD + q, e * P:(e + 1) * P], wt_raw[l][:, q, :],
                                                start=(q == 0), stop=(q == KD - 1))
                last.then_inc(weight_product, 1)

            with pe.Fori(0, LAYERS) as layer:
                def pair(k, b):
                    if has_pair(k, b, 0):
                        pe.wait_ge(rows_loaded[b], layer * (PAIRS // PAIR_ROUND * 16) + k * 16 + 16)
                        for t in range(2):
                            for e in range(KD):
                                at = (t * KD + e) * P
                                last = nc.tensor.transpose(feature_bank[b % 2][:, at:at + P],
                                                           rows[:, b, t, e * P:(e + 1) * P], ident[:, :])
                        last.then_inc(rows_turned, 1)
                    if not has_pair(k, b, 1):
                        return
                    a = (b - 1) % 2
                    h = pair_features(a)
                    pe.wait_ge(feature_lo, pairs_done(layer, k, b, 1))
                    for t in range(2):
                        for e in range(KD):
                            for i, (w, m) in enumerate(PRODUCTS):
                                last = nc.tensor.matmul(
                                    value_bank[a][:, t * D:(t + 1) * D],
                                    h[:, t, e, w, :], value_weight[:, e, m, :],
                                    start=(e == 0 and i == 0), stop=(e == KD - 1 and i == 2))
                    last.then_inc(value_product, 1)
                    for d in range(KD):
                        for e in range(KD):
                            for i, (w, m) in enumerate(PRODUCTS):
                                last = nc.tensor.matmul(
                                    score_bank[a][:, d * 2 * P:(d + 1) * 2 * P],
                                    score_weight[:, e, w, d * P:(d + 1) * P], h[:, :, e, m, :],
                                    start=(e == 0 and i == 0), stop=(e == KD - 1 and i == 2))
                    last.then_inc(key_product, 1)

                pe.wait_ge(weights_ready, (layer + 1) * 32)
                all_pairs(pe, pair, 1)

                def score(k, c):
                    b = (c // CHUNKS) % 2
                    if c % CHUNKS == 0:
                        pe.wait_ge(query_loaded[b], layer * (16 * PAIRS) + k * 16 + 16)
                    if later(k, c, 0, 4):
                        pe.wait_ge(copied, done(layer, k, c, 4))
                    elif c < 2:
                        pe.wait_ge(key_lo, (layer + 1) * PAIRS - 1 + c)
                    elif c == 2:
                        pe.wait_ge(value_lo, (layer + 1) * PAIRS)
                    col = (c % CHUNKS) * CW
                    for e in range(KD):
                        for i, (a, m) in enumerate(PRODUCTS):
                            last = nc.tensor.matmul(score_bank[c % 4][:, :], query[:, b, e, a, :],
                                                    keys[:, e, m, col:col + CW],
                                                    start=(e == 0 and i == 0), stop=(e == KD - 1 and i == 2))
                    last.then_inc(scored, 1)

                def times_values(k, c):
                    u = (c - LAG_VALUE) % ROUND
                    t = u // CHUNKS
                    first, end = u % CHUNKS == 0, u % CHUNKS == CHUNKS - 1
                    pe.wait_ge(split_lo, done(layer, k, c, LAG_VALUE))
                    if first and later(k, c, LAG_VALUE, ROUND):
                        pe.wait_ge(h_ready, (layer + 1) * TILES + tile(k, c - LAG_VALUE) - 1)
                    for j in range(BLOCKS):
                        row = (u % CHUNKS) * BLOCKS + j
                        nc.tensor.matmul(sum_bank[t][:, :], split[:, u % 4, j * P:(j + 1) * P],
                                         values[:, row, :, :].rearrange("p s d -> p (s d)"),
                                         start=(first and j == 0), stop=False)
                        last = nc.tensor.matmul(sum_bank[t][:, 0:D],
                                                split[:, u % 4, CW + j * P:CW + (j + 1) * P],
                                                values[:, row, HI, :],
                                                start=False, stop=(end and j == BLOCKS - 1))
                    last.then_inc(summed, 1)

                def step(k, c):
                    if inside(k, c, 0):
                        score(k, c)
                    if inside(k, c, LAG_VALUE):
                        times_values(k, c)
                all_steps(pe, step)

        @block.vector
        def _(dve):
            n = [0]

            def link(instruction):
                n[0] += 1
                instruction.then_inc(stats_step, 1)
                dve.wait_ge(stats_step, n[0])

            for i in range(4):
                g = slice(i * (TILES // 4), (i + 1) * (TILES // 4))
                dve.wait_ge(x_loaded[i], 16)
                for t in range(g.start, g.stop):
                    nc.vector.bn_stats(bn[:, t, :], x_all[:, t, :]).then_inc(stats_step, 1)
                n[0] += TILES // 4
                dve.wait_ge(stats_step, n[0])
                nc.vector.tensor_tensor(mean[:, g], bn[:, g, 1], bn[:, g, 4], ALU.add).then_inc(stats_step, 1)
                nc.vector.tensor_tensor(tmp[:, g], bn[:, g, 1], bn[:, g, 4], ALU.subtract).then_inc(stats_step, 1)
                n[0] += 2
                link(nc.vector.tensor_tensor(var[:, g], bn[:, g, 2], bn[:, g, 5], ALU.add))
                nc.vector.tensor_tensor(tmp[:, g], tmp[:, g], tmp[:, g], ALU.mult).then_inc(stats_step, 1)
                n[0] += 1
                link(nc.vector.tensor_scalar(var[:, g], var[:, g], 1.0 / D, EPS, ALU.mult, ALU.add))
                link(nc.vector.scalar_tensor_tensor(out=var[:, g], in0=tmp[:, g], scalar=0.25,
                                                    in1=var[:, g], op0=ALU.mult, op1=ALU.add))
                nc.vector.reciprocal(rstd[:, g], var[:, g]).then_inc(var_ready, 1)
                dve.wait_ge(sqrt_ready, i + 1)
                link(nc.vector.tensor_tensor(tmp[:, g], rstd[:, g], rstd[:, g], ALU.mult))
                link(nc.vector.tensor_tensor(tmp[:, g], tmp[:, g], var[:, g], ALU.mult))
                link(nc.vector.tensor_scalar(tmp[:, g], tmp[:, g], -0.5, 1.5, ALU.mult, ALU.add))
                link(nc.vector.tensor_tensor(rstd[:, g], rstd[:, g], tmp[:, g], ALU.mult))
                nc.vector.scalar_tensor_tensor(out=shift[:, g], in0=mean[:, g], scalar=-0.5, in1=rstd[:, g],
                                               op0=ALU.mult, op1=ALU.mult).then_inc(scale_ready, 1)
                if i == 1:
                    for l in range(LAYERS):
                        dve.wait_ge(weight_hi, l * 2 + 1)
                        nc.vector.tensor_tensor(value_weights[l][:, :, LO, :], wv_raw[l],
                                                value_weights[l][:, :, HI, :].bitcast(F32), ALU.subtract
                                                ).then_inc(weight_lo if l else weights_ready, 1 if l else 16)
                        dve.wait_ge(weight_hi, l * 2 + 2)
                        nc.vector.tensor_tensor(score_weights[l][:, :, LO, :],
                                                sum_bank[l][:, :].rearrange("p (e d) -> p e d", e=KD),
                                                score_weights[l][:, :, HI, :].bitcast(F32), ALU.subtract
                                                ).then_inc(weight_lo if l else weights_ready, 1 if l else 16)

            with dve.Fori(0, LAYERS) as layer:
                def pair(k, b):
                    if has_pair(k, b, 0):
                        h = split[:, 2 + b % 2, :].rearrange("p (t s r) -> p t s r", t=2 * KD, s=2)
                        dve.wait_ge(feature_hi, pairs_done(layer, k, b, 0))
                        nc.vector.tensor_tensor(h[:, :, LO, :],
                                                feature_bank[b % 2][:, :].rearrange("p (t r) -> p t r", r=P),
                                                h[:, :, HI, :].bitcast(F32),
                                                ALU.subtract).then_inc(feature_lo, 1)
                    if has_pair(k, b, 1):
                        a = (b - 1) % 2
                        dve.wait_ge(value_hi, pairs_done(layer, k, b, 1))
                        at = bass.ds(k * (2 * PAIR_ROUND) + 2 * (b - 1), 2)
                        nc.vector.tensor_tensor(values[:, at, LO, :],
                                                value_bank[a][:, :].rearrange("p (t d) -> p t d", t=2),
                                                values[:, at, HI, :].bitcast(F32),
                                                ALU.subtract).then_inc(value_lo, 1)
                        dve.wait_ge(key_hi, pairs_done(layer, k, b, 1))
                        nc.vector.tensor_tensor(pair_keys(LO, k, b - 1), by_run(score_bank[a]),
                                                pair_keys(HI, k, b - 1).bitcast(F32),
                                                ALU.subtract).then_inc(key_lo, 1)

                all_pairs(dve, pair, 1)

                def copy(k, c):
                    t = (c // CHUNKS) % 2
                    dve.wait_ge(scored, done(layer, k, c, 0))
                    if later(k, c, 0, ROUND):
                        dve.wait_ge(shuffled[c // 2 % 2], shuffles_done(layer, k - 1, c))
                    nc.vector.tensor_scalar(scores[:, c, :], score_bank[c % 4][:, :], 1.0, None, ALU.mult,
                                            ALU.max, accum_out=chunk_max[:, t, c % CHUNKS:c % CHUNKS + 1]
                                            ).then_inc(copied, 1)
                    if c % CHUNKS == CHUNKS - 1:
                        dve.wait_ge(copied, done(layer, k, c, 0))
                        nc.vector.tensor_reduce(neg_max[:, t:t + 1], chunk_max[:, t, :], AX.X, ALU.max,
                                                negate=True).then_inc(maxed, 1)

                def turn(k, c):
                    u = (c - LAG_TURN) % ROUND
                    dve.wait_ge(masked, done(layer, k, c, LAG_TURN))
                    nc.vector.transpose(scores[:, u, :], scores[:, u, :]).then_inc(turned, 1)

                def split_turned(k, c):
                    u = (c - LAG_SPLIT) % ROUND
                    dve.wait_ge(split_hi, done(layer, k, c, LAG_SPLIT))
                    nc.vector.tensor_tensor(split[:, u % 4, CW:2 * CW].rearrange("p (j a i) -> p j a i", a=RUNS, i=Q),
                                            turned_chunk(u),
                                            split[:, u % 4, 0:CW].bitcast(F32).rearrange(
                                                "p (j a i) -> p j a i", a=RUNS, i=Q),
                                            ALU.subtract).then_inc(split_lo, 1)

                def invert_sum(k, c, lag):
                    b = ((c - lag) // CHUNKS) % 2
                    T = layer * TILES + tile(k, c - lag)
                    dve.wait_ge(expd, done(layer, k, c, lag - CHUNKS + 1))
                    nc.vector.tensor_reduce(row_sum[:, :], chunk_sum[:, b, :], AX.X, ALU.add
                                            ).then_inc(sum_ready, 1)
                    dve.wait_ge(sum_ready, T + 1)
                    nc.vector.reciprocal(inv_sum[:, :], row_sum[:, :]).then_inc(inv_ready, 1)

                def finish(k, c, lag):
                    b = ((c - lag) // CHUNKS) % 2
                    t = tile(k, c - lag)
                    T = layer * TILES + t
                    dve.wait_ge(low_ready, T + 1)
                    dve.wait_ge(h_stored[b], (layer + 1) * (16 * PAIRS) + k * 16 + 16 * ((c - lag) // ROUND))
                    nc.vector.scalar_tensor_tensor(out=finished[:, b, :], in0=sum_bank[b][:, 0:D],
                                                   scalar=inv_sum[:, :], in1=low_part[:, :],
                                                   op0=ALU.mult, op1=ALU.add).then_inc(finish_step, 1)
                    dve.wait_ge(residual_loaded, (T + 1) * 32)
                    dve.wait_ge(finish_step, T * 3 + 1)
                    nc.vector.tensor_tensor(finished[:, b, :], finished[:, b, :], residual[:, :],
                                            ALU.add).then_inc(finish_step, 1)
                    dve.wait_ge(finish_step, T * 3 + 2)
                    nc.vector.scalar_tensor_tensor(out=finished[:, b, :], in0=finished[:, b, :],
                                                   scalar=SLOPE, in1=finished[:, b, :],
                                                   op0=ALU.mult, op1=ALU.max).then_inc(finish_step, 1)
                    dve.wait_ge(finish_step, T * 3 + 3)
                    nc.vector.tensor_tensor(finished[:, b, :], finished[:, b, :], addend[:, :],
                                            ALU.add).then_inc(h_ready, 1)

                def step(k, c):
                    if inside(k, c, LAG_TURN):
                        turn(k, c)
                    if inside(k, c, LAG_SPLIT):
                        split_turned(k, c)
                    if inside(k, c, 0):
                        copy(k, c)
                    lag = CHUNKS - 1 + LAG_FINISH
                    if (c + 1 - lag) % CHUNKS == 0 and inside(k, c + 1, lag):
                        invert_sum(k, c + 1, lag)
                    if (c - lag) % CHUNKS == 0 and inside(k, c, lag):
                        finish(k, c, lag)
                all_steps(dve, step)

        @block.scalar
        def _(act):
            for i in range(4):
                g = slice(i * (TILES // 4), (i + 1) * (TILES // 4))
                act.wait_ge(var_ready, i + 1)
                nc.scalar.activation(rstd[:, g], rstd[:, g], ACT.Sqrt).then_inc(sqrt_ready, 1)
                act.wait_ge(scale_ready, i + 1)
                for t in range(g.start, g.stop):
                    nc.scalar.activation(x_all[:, t, :], x_all[:, t, :], ACT.Relu, bias=shift[:, t:t + 1],
                                         scale=rstd[:, t:t + 1]).then_inc(h_ready, 1)
                if i == 0:
                    act.wait_ge(weights_loaded, LAYERS * 32)
                    for l in range(LAYERS):
                        nc.scalar.activation(value_weights[l][:, :, HI, :], wv_raw[l], ACT.Copy
                                             ).then_inc(weight_hi, 1)
                        act.wait_ge(weight_product, l + 1)
                        nc.scalar.activation(score_weights[l][:, :, HI, :],
                                             sum_bank[l][:, :].rearrange("p (e d) -> p e d", e=KD),
                                             ACT.Copy).then_inc(weight_hi, 1)
            act.wait_ge(weight_lo, 2 * (LAYERS - 1))
            for entry in range(LAYERS):
                l = min(entry + 1, LAYERS - 1)
                act.dma_start(weight_dram[entry, 0, :, :], split[:, l, :].bitcast(F32)
                              ).then_inc(weights_stored, 16)
                act.dma_start(weight_dram[entry, 1, :, :].rearrange("p (a x) -> p a x", a=RUNS),
                              turned_ring[:, l, :, :].bitcast(F32)).then_inc(weights_stored, 16)
            nc.scalar.preload_act_table(ACT.Exp)

            with act.Fori(0, LAYERS) as layer:
                def pair(k, b):
                    if has_pair(k, b, 0):
                        h = split[:, 2 + b % 2, :].rearrange("p (t s r) -> p t s r", t=2 * KD, s=2)
                        act.wait_ge(rows_turned, pairs_done(layer, k, b, 0))
                        if after(k, b, 0, 2):
                            act.wait_ge(feature_stored[b % 2], layer * (8 * PAIRS) + k * (8 * PAIR_ROUND)
                                        + 16 * (b // 2))
                        nc.scalar.activation(h[:, :, HI, :],
                                             feature_bank[b % 2][:, :].rearrange("p (t r) -> p t r", r=P),
                                             ACT.Copy).then_inc(feature_hi, 1)
                    if has_pair(k, b, 1):
                        a = (b - 1) % 2
                        act.wait_ge(value_product, pairs_done(layer, k, b, 1))
                        nc.scalar.activation(values[:, bass.ds(k * (2 * PAIR_ROUND) + 2 * (b - 1), 2), HI, :],
                                             value_bank[a][:, :].rearrange("p (t d) -> p t d", t=2),
                                             ACT.Copy).then_inc(value_hi, 1)
                        act.wait_ge(key_product, pairs_done(layer, k, b, 1))
                        nc.scalar.activation(pair_keys(HI, k, b - 1), by_run(score_bank[a]), ACT.Copy
                                             ).then_inc(key_hi, 1)

                all_pairs(act, pair, 1)
                act.wait_ge(weights_stored, LAYERS * 32)
                for b in range(2):
                    act.wait_ge(feature_stored[b], (layer + 1) * (8 * PAIRS))

                def exponentials(k, c):
                    u = (c - LAG_EXP) % ROUND
                    t = u // CHUNKS
                    if u % CHUNKS == 0:
                        act.wait_ge(maxed, layer * TILES + tile(k, c - LAG_EXP) + 1)
                    nc.scalar.activation(scores[:, u, :], scores[:, u, :], ACT.Exp, bias=neg_max[:, t:t + 1],
                                         accum_out=chunk_sum[:, t, u % CHUNKS:u % CHUNKS + 1]
                                         ).then_inc(expd, 1)

                def split_turned(k, c):
                    u = (c - LAG_SPLIT) % ROUND
                    if u % 2 == 0:
                        act.wait_ge(shuffled[u // 2 % 2], shuffles_done(layer, k + (c - LAG_SPLIT) // ROUND, u))
                    if later(k, c, LAG_SPLIT, 4):
                        act.wait_ge(summed, done(layer, k, c, LAG_SPLIT + 4))
                    nc.scalar.activation(split[:, u % 4, 0:CW].rearrange("p (j a i) -> p j a i", a=RUNS, i=Q),
                                         turned_chunk(u), ACT.Copy).then_inc(split_hi, 1)

                def scale_low(k, c, lag):
                    b = ((c - lag) // CHUNKS) % 2
                    T = layer * TILES + tile(k, c - lag)
                    act.wait_ge(summed, done(layer, k, c, LAG_FINISH))
                    act.wait_ge(inv_ready, T + 1)
                    nc.scalar.activation(low_part[:, :], sum_bank[b][:, D:2 * D], ACT.Copy,
                                         scale=inv_sum[:, :]).then_inc(low_ready, 1)

                def store(k, c, lag):
                    b = ((c - lag) // CHUNKS) % 2
                    t = tile(k, c - lag)
                    act.wait_ge(h_ready, (layer + 1) * TILES + t + 1)
                    act.dma_start(out_tiles[bass.ds(t, 1), :, :].rearrange("o p d -> p (o d)"),
                                  finished[:, b, :]).then_inc(h_stored[b], 16)

                def step(k, c):
                    if inside(k, c, LAG_SPLIT):
                        split_turned(k, c)
                    if inside(k, c, LAG_EXP):
                        exponentials(k, c)
                    lag = CHUNKS - 1 + LAG_FINISH
                    if (c - lag) % CHUNKS == 0 and inside(k, c, lag):
                        scale_low(k, c, lag)
                    lag += 1
                    if (c - lag) % CHUNKS == 0 and inside(k, c, lag):
                        store(k, c, lag)
                all_steps(act, step)

        @block.gpsimd
        def _(pool):
            nc.gpsimd.memset(ident[:, :], 0.0).then_inc(ident_made, 1)
            pool.wait_ge(ident_made, 1)
            nc.gpsimd.affine_select(out=ident[:, :], in_=ident[:, :], compare_op=ALU.not_equal, fill=1.0,
                                    base=0, pattern=[[-1, P]], channel_multiplier=1).then_inc(ident_made, 1)

            with pool.Fori(0, LAYERS) as layer:
                def step(k, c):
                    if not inside(k, c, LAG_EXP):
                        return
                    u = (c - LAG_EXP) % ROUND
                    slot = (u // 2) % ADJ_SLOTS
                    pool.wait_ge(expd, done(layer, k, c, LAG_EXP))
                    if u % 2 == 0:
                        pool.wait_ge(adj_loaded[slot], layer * (32 * ROUNDS) + k * 32
                                     + 16 * ((c - LAG_EXP) // (2 * ADJ_SLOTS) + 1))
                    half = (u % 2) * CW
                    nc.gpsimd.tensor_tensor(scores[:, u, :], scores[:, u, :],
                                            adj_ring[:, slot, half:half + CW], ALU.mult).then_inc(masked, 1)

                all_steps(pool, step)


def kernel(x, adj, L0_gnn_W_stack):
    import numpy as np
    import concourse.bacc as bacc
    from concourse.bass_utils import run_bass_kernel_spmd

    x, adj, w = (np.asarray(a) for a in (x, adj, L0_gnn_W_stack))
    n, d = x.shape
    arrays = {
        "x_padded": np.ascontiguousarray(np.concatenate([np.zeros((P, d), x.dtype), x])),
        "adj": np.ascontiguousarray(
            adj.reshape(n, n // 1024, 8, 32, 4).transpose(0, 1, 4, 2, 3).reshape(n, n)),
        "w_value": np.ascontiguousarray(w[:, :, 0:d]),
        "w_transposed": np.ascontiguousarray(w.transpose(0, 2, 1)),
    }
    nc = bacc.Bacc("TRN2", target_bir_lowering=False, num_devices=1, dynamic_dma_scratch_size=1024)
    ins = [nc.dram_tensor(n, a.shape, mybir.dt.from_np(a.dtype), kind="ExternalInput").ap()
           for n, a in arrays.items()]
    out = nc.dram_tensor("out", x.shape, mybir.dt.from_np(x.dtype), kind="ExternalOutput").ap()
    gnn_kernel(nc, *ins, out)
    result = run_bass_kernel_spmd(nc, [arrays], core_ids=[0])
    return result.results[0]["out"]
```

```python
from contextlib import ExitStack

import concourse.bass as bass
from concourse import mybir

F32 = mybir.dt.float32
F32R = mybir.dt.float32r
ALU = mybir.AluOpType
ACT = mybir.ActivationFunctionType
AX = mybir.AxisListType

P = 128
HI, LO = 0, 1
EPS = 1e-5
SLOPE = 0.01
PRODUCTS = ((HI, HI), (HI, LO), (LO, HI))


def gnn_kernel(nc, x_padded, adj, w_value, w_transposed, out):
    N, D = out.shape
    LAYERS = w_value.shape[0]
    TILES = N // P
    CW = 512
    CHUNKS = N // CW
    STEPS = TILES * CHUNKS
    BLOCKS = CW // P
    KD = D // P
    ROUND = 2 * CHUNKS
    ROUNDS = STEPS // ROUND
    PAIRS = TILES // 2
    Q = 32
    RUNS = P // Q
    GROUP = 2 * CW
    RUN = GROUP // RUNS
    PAIR_ROUND = GROUP // (2 * P)
    LAG_EXP = CHUNKS
    LAG_TURN = CHUNKS + 1
    LAG_SHUFFLE = CHUNKS + 4
    LAG_SPLIT = CHUNKS + 5
    LAG_VALUE = LAG_SPLIT + 1
    LAG_FINISH = LAG_VALUE + 1
    LAG_RESIDUAL = LAG_FINISH + 2
    TAIL = ROUND
    LEAD = 4
    ADJ_SLOTS = 4

    POOL_TILES, DVE_TILES = (2, 0, 0, 1), (2, 2, 2, 3)
    QUARTERS = [slice(i * (TILES // 4), (i + 1) * (TILES // 4)) for i in range(4)]

    def quarter_tiles(i):
        end = QUARTERS[i].stop
        return QUARTERS[i].start, end - POOL_TILES[i] - DVE_TILES[i], end - POOL_TILES[i]

    assert CHUNKS % 2 == 0 and PAIRS % PAIR_ROUND == 0 and QUARTERS[0].stop >= 2 * PAIR_ROUND
    adj_rows = adj.rearrange("(t p) n -> t p n", p=P)
    x_tiles = x_padded.rearrange("(t p) d -> t p d", p=P)
    out_tiles = out.rearrange("(t p) d -> t p d", p=P)
    feature_dram = nc.dram_tensor("feature_dram", [TILES, P, KD * 2 * P], F32, kind="Internal").ap()
    weight_dram = nc.dram_tensor("weight_dram", [LAYERS - 1, 2, P, KD * 2 * D], F32, kind="Internal").ap()

    with ExitStack() as ctx:
        def sb(name, shape, dt=F32):
            return ctx.enter_context(nc.sbuf_tensor(name, shape, dt))

        def ps(name):
            return ctx.enter_context(nc.psum_tensor(name, [P, CW], F32))

        def sem(name):
            return ctx.enter_context(nc.semaphore(name))

        keys = sb("keys", [P, KD, 2, N], F32R)
        turned_ring = sb("turned_ring", [P, 2, RUNS, RUN], F32R)
        values = sb("values", [P, TILES, 2, D], F32R)
        scores = sb("scores", [P, ROUND, CW])
        adj_ring = sb("adj_ring", [P, ADJ_SLOTS, 2 * CW])
        split = sb("split", [P, 4, 2 * CW], F32R)
        query = sb("query", [P, 2, KD, 2, P], F32R)
        rows = sb("rows", [P, PAIR_ROUND, 2, D])
        finished = sb("finished", [P, 2, D])
        residual = sb("residual", [P, D])
        addend = sb("addend", [P, D])
        low_part = sb("low_part", [P, D])
        ident = sb("ident", [P, P])
        chunk_max = sb("chunk_max", [P, 2, CHUNKS])
        neg_max = sb("neg_max", [P, 2])
        chunk_sum = sb("chunk_sum", [P, 2, CHUNKS])
        row_sum = sb("row_sum", [P, 1])
        inv_sum = sb("inv_sum", [P, 1])
        bn = sb("bn", [P, TILES, 6])
        mean = sb("mean", [P, TILES])
        rstd = sb("rstd", [P, TILES])
        var = sb("var", [P, TILES])
        tmp = sb("tmp", [P, TILES])
        shift = sb("shift", [P, TILES])
        x_all = scores[:, :, :].rearrange("p a (b d) -> p (a b) d", d=D)
        wt_raw = [adj_ring[:, 2 * l, :].rearrange("p (q d) -> p q d", d=D) for l in range(LAYERS)]
        wv_raw = [adj_ring[:, 2 * l + 1, 0:KD * D].rearrange("p (q d) -> p q d", d=D) for l in range(LAYERS)]

        score_weights = [split[:, l, :].rearrange("p (e s d) -> p e s d", e=KD, s=2) for l in range(LAYERS)]
        value_weights = [turned_ring[:, l, :, :].rearrange("p a (s d) -> p (a s) d", d=D).rearrange(
            "p (e s) d -> p e s d", e=KD) for l in range(LAYERS)]
        score_weight, value_weight = score_weights[0], value_weights[0]

        keys_by_run = keys[:, :, :, :].rearrange("p d s (g b x) -> p d s g b x", b=RUNS, x=RUN)

        def pair_keys(part, k, b):
            u = b % PAIR_ROUND
            return keys_by_run[:, :, part, bass.ds(k + b // PAIR_ROUND, 1), :, 2 * Q * u:2 * Q * (u + 1)
                               ].rearrange("p d o b x -> p d (o b) x")

        def turned_chunk(u):
            return turned_ring[:, u // 2 % 2, :, u % 2 * (RUN // 2):(u % 2 + 1) * (RUN // 2)].bitcast(F32).rearrange(
                "p a (j i) -> p j a i", i=Q)

        def by_run(bank):
            return bank[:, :].rearrange("p (d x b) -> p d b x", d=KD, b=RUNS)

        def pair_features(slot):
            return split[:, 2 + slot, :].rearrange("p (t e s r) -> p t e s r", t=2, e=KD, s=2)

        score_bank = [ps(f"score_bank{i}") for i in range(4)]
        value_bank = score_bank[2:4]
        sum_bank = [ps("sum_bank0"), ps("sum_bank1")]
        feature_bank = [ps("feature_bank0"), ps("feature_bank1")]

        ident_made = sem("ident_made")
        x_loaded = [sem(f"x_loaded{i}") for i in range(4)]
        stats_ready = sem("stats_ready")
        norm_step = sem("norm_step")
        var_ready = sem("var_ready")
        inv_var_ready = sem("inv_var_ready")
        sqrt_ready = sem("sqrt_ready")
        scale_ready = sem("scale_ready")
        shifted = sem("shifted")
        weights_loaded = sem("weights_loaded")
        weight_product = sem("weight_product")
        weight_hi = sem("weight_hi")
        weight_lo = sem("weight_lo")
        weights_stored = sem("weights_stored")
        weights_ready = sem("weights_ready")
        rows_loaded = [sem(f"rows_loaded{i}") for i in range(PAIR_ROUND)]
        rows_turned = sem("rows_turned")
        feature_hi = sem("feature_hi")
        feature_lo = sem("feature_lo")
        feature_stored = [sem("feature_stored0"), sem("feature_stored1")]
        key_product = sem("key_product")
        key_hi = sem("key_hi")
        key_lo = sem("key_lo")
        value_product = sem("value_product")
        value_hi = sem("value_hi")
        value_lo = sem("value_lo")
        adj_loaded = [sem(f"adj_loaded{i}") for i in range(ADJ_SLOTS)]
        query_loaded = [sem("query_loaded0"), sem("query_loaded1")]
        residual_loaded = sem("residual_loaded")
        scored = sem("scored")
        copied = sem("copied")
        maxed = sem("maxed")
        expd = sem("expd")
        masked = sem("masked")
        turned = sem("turned")
        shuffled = [sem("shuffled0"), sem("shuffled1")]
        split_hi = sem("split_hi")
        split_lo = sem("split_lo")
        summed = sem("summed")
        sum_ready = sem("sum_ready")
        inv_ready = sem("inv_ready")
        low_ready = sem("low_ready")
        finish_step = sem("finish_step")
        normalised = [sem(f"normalised{i}") for i in range(4)]
        h_ready = sem("h_ready")
        h_stored = [sem("h_stored0"), sem("h_stored1")]

        def inside(k, c, lag):
            if isinstance(k, int):
                return 0 <= ROUND * k + c - lag < STEPS
            assert -ROUND <= c - lag < ROUND
            return True

        def done(layer, k, c, lag):
            return layer * STEPS + k * ROUND + (c - lag + 1)

        def later(k, c, lag, n):
            return not isinstance(k, int) or ROUND * k + c - lag >= n

        def tile(k, c):
            return k * 2 + c // CHUNKS

        def finished_tiles(layer, n):
            return layer * TILES + n + 1

        def all_steps(eng, step):
            for c in range(ROUND):
                step(0, c)
            with eng.Fori(1, ROUNDS) as k:
                for c in range(ROUND):
                    step(k, c)
            for c in range(TAIL):
                step(ROUNDS, c)

        def all_pairs(eng, step, lag):
            for b in range(PAIR_ROUND):
                step(0, b)
            with eng.Fori(1, PAIRS // PAIR_ROUND) as k:
                for b in range(PAIR_ROUND):
                    step(k, b)
            for b in range(lag):
                step(PAIRS // PAIR_ROUND, b)

        def after(k, b, lag, n):
            return not isinstance(k, int) or PAIR_ROUND * k + b - lag >= n

        def has_pair(k, b, lag):
            return not isinstance(k, int) or 0 <= PAIR_ROUND * k + b - lag < PAIRS

        def pairs_done(layer, k, b, lag):
            return layer * PAIRS + k * PAIR_ROUND + (b - lag + 1)

        def shuffles_done(layer, k, u):
            return layer * (STEPS // 4 * 64) + k * (ROUND // 4 * 64) + 64 * (u // 4 + 1)

        block = ctx.enter_context(nc.Block())

        @block.sync
        def _(sp):
            n = TILES // 4

            def load_x(i):
                sp.dma_start(x_all[:, i * n:(i + 1) * n, :],
                             x_tiles[1 + i * n:1 + (i + 1) * n, :, :].rearrange("t p d -> p t d")
                             ).then_inc(x_loaded[i], 16)

            load_x(0)
            for l in range(LAYERS):
                sp.dma_start(wt_raw[l], w_transposed[l, :, :].rearrange("(q p) d -> p q d", p=P)
                             ).then_inc(weights_loaded, 16)
                sp.dma_start(wv_raw[l], w_value[l, :, :].rearrange("(q p) d -> p q d", p=P)
                             ).then_inc(weights_loaded, 16)
            for i in range(1, 4):
                load_x(i)

            def load_rows(b, first_tile):
                sp.dma_start(rows[:, b, :, :], out_tiles[bass.ds(first_tile, 2), :, :].rearrange(
                    "t p d -> p t d")).then_inc(rows_loaded[b], 16)

            def store_quarter(i):
                sp.wait_ge(normalised[i], TILES // 4)
                for b in range(2):
                    tiles = slice(QUARTERS[i].start + b, QUARTERS[i].stop, 2)
                    sp.dma_start(out_tiles[tiles, :, :].rearrange("t p d -> p t d"), x_all[:, tiles, :]
                                 ).then_inc(h_stored[b], 16 * PAIRS // 4)

            store_quarter(0)
            for b in range(2):
                sp.wait_ge(h_stored[b], 16 * PAIRS // 4)
            for b in range(PAIR_ROUND):
                load_rows(b, 2 * b)
            store_quarter(1)
            store_quarter(2)
            store_quarter(3)
            sp.wait_ge(weight_lo, 2 * (LAYERS - 1))
            for l in range(1, LAYERS):
                sp.dma_start(weight_dram[l - 1, 0, :, :], split[:, l, :].bitcast(F32)
                             ).then_inc(weights_stored, 16)
                sp.dma_start(weight_dram[l - 1, 1, :, :].rearrange("p (a x) -> p a x", a=RUNS),
                             turned_ring[:, l, :, :].bitcast(F32)).then_inc(weights_stored, 16)

            with sp.Fori(0, LAYERS) as layer:
                def load_adj(k, c, lag):
                    u = (c - lag) % ROUND
                    slot = u // 2 % ADJ_SLOTS
                    cols = slice(u % CHUNKS * CW, (u % CHUNKS + 2) * CW)
                    sp.dma_start(adj_ring[:, slot, :],
                                 adj_rows[bass.ds(tile(k, c - lag), 1), :, cols].rearrange(
                                     "o p n -> p (o n)")).then_inc(adj_loaded[slot], 16)

                def load_query(k, c):
                    b = c // CHUNKS % 2
                    sp.dma_start(query[:, b, :, :, :].rearrange("p e s r -> p (e s r)").bitcast(F32),
                                 feature_dram[bass.ds(tile(k, c), 1), :, :].rearrange(
                                     "o p d -> p (o d)")).then_inc(query_loaded[b], 16)

                def pair(k, b):
                    if has_pair(k, b, 0) and after(k, b, 0, PAIR_ROUND):
                        sp.wait_ge(rows_turned, pairs_done(layer, k, b, PAIR_ROUND))
                        load_rows(b, k * (2 * PAIR_ROUND) + 2 * b)
                    if has_pair(k, b, 2):
                        sp.wait_ge(feature_lo, pairs_done(layer, k, b, 2))
                        sp.dma_start(feature_dram[bass.ds(k * (2 * PAIR_ROUND) + 2 * (b - 2), 2), :, :
                                                  ].rearrange("t p f -> p t f"),
                                     split[:, 2 + b % 2, :].bitcast(F32).rearrange("p (t f) -> p t f", t=2)
                                     ).then_inc(feature_stored[b % 2], 16)

                for b in range(PAIR_ROUND):
                    pair(0, b)
                first_stored = layer * (8 * PAIRS) + 16
                sp.to_reg(first_stored)
                for b in range(2):
                    sp.wait_ge(h_stored[b], (layer + 1) * (16 * PAIRS))
                sp.wait_ge(feature_stored[0], first_stored)
                load_query(0, 0)
                load_query(0, CHUNKS)
                with sp.Fori(1, PAIRS // PAIR_ROUND) as k:
                    for b in range(PAIR_ROUND):
                        pair(k, b)
                for b in range(2):
                    pair(PAIRS // PAIR_ROUND, b)
                for b in range(2):
                    sp.wait_ge(feature_stored[b], (layer + 1) * (8 * PAIRS))
                sp.wait_ge(weights_stored, (LAYERS - 1) * 32)
                for c in range(0, 2 * ADJ_SLOTS, 2):
                    load_adj(0, c, 0)

                def next_layer():
                    for b in range(2):
                        sp.wait_ge(h_stored[b], (layer + 1) * (16 * PAIRS) + 16 * PAIR_ROUND)
                    for b in range(PAIR_ROUND):
                        load_rows(b, 2 * b)
                    sp.wait_ge(summed, (layer + 1) * STEPS - 2)
                    entry = 0 if LAYERS == 2 else layer % (LAYERS - 1)
                    for which, target in enumerate((
                            split[:, 0, :], turned_ring[:, 0, :, :].rearrange("p a x -> p (a x)"))):
                        sp.dma_start(target.bitcast(F32), weight_dram[bass.ds(entry, 1), which, :, :].rearrange(
                            "o p w -> p (o w)")).then_inc(weights_ready, 16)

                def step(k, c):
                    if (c - LEAD) % 2 == 0 and inside(k, c, LEAD) and later(k, c, LEAD, 2 * ADJ_SLOTS):
                        sp.wait_ge(masked, done(layer, k, c, LEAD + 2 * ADJ_SLOTS - 1))
                        load_adj(k, c, LEAD)
                    if c % CHUNKS == 0 and inside(k, c, 0) and later(k, c, 0, 2 * CHUNKS):
                        sp.wait_ge(scored, done(layer, k, c, CHUNKS + 1))
                        load_query(k, c)
                    if inside(k, c, LAG_SHUFFLE) and (c - LAG_SHUFFLE) % 2 == 1:
                        u = (c - LAG_SHUFFLE) % ROUND
                        slot = u // 2 % 2
                        group_before = done(layer, k, c, LAG_SHUFFLE + 4)
                        if later(k, c, LAG_SHUFFLE, 4):
                            sp.to_reg(group_before)
                        sp.wait_ge(turned, done(layer, k, c, LAG_SHUFFLE))
                        if later(k, c, LAG_SHUFFLE, 4):
                            sp.wait_ge(split_lo, group_before)
                        for a in range(RUNS):
                            sp.dma_start(turned_ring[:, slot, a, :].bitcast(F32),
                                         scores[a * Q:(a + 1) * Q, u - 1:u + 1, :]
                                         ).then_inc(shuffled[slot], 16)
                    lag = LAG_RESIDUAL
                    if (c - lag) % CHUNKS == 0 and inside(k, c, lag):
                        t = tile(k, c - lag)
                        b = ((c - lag) // CHUNKS) % 2
                        tiles_before = finished_tiles(layer, t)
                        sp.to_reg(tiles_before)
                        sp.wait_ge(h_stored[b], layer * (16 * PAIRS) + k * 16
                                   + 16 * ((c - lag) // ROUND + 1))
                        sp.wait_ge(h_ready, tiles_before)
                        sp.dma_start(residual[:, :], out_tiles[bass.ds(t, 1), :, :].rearrange(
                            "o p d -> p (o d)")).then_inc(residual_loaded, 16)
                        sp.dma_start(addend[:, :], x_tiles[bass.ds(layer * (t + 1), 1), :, :].rearrange(
                            "o p d -> p (o d)")).then_inc(residual_loaded, 16)

                all_steps(sp, step)
                next_layer()
                sp.wait_ge(h_ready, finished_tiles(layer, TILES))
                sp.dma_start(out_tiles[TILES - 1, :, :], finished[:, 1, :]).then_inc(h_stored[1], 16)

            for b in range(2):
                sp.wait_ge(h_stored[b], (LAYERS + 1) * PAIRS * 16)
            for b in range(PAIR_ROUND):
                sp.wait_ge(rows_loaded[b], (LAYERS * PAIRS // PAIR_ROUND + 1) * 16)
            sp.wait_ge(weights_ready, (LAYERS + 1) * 32)
            sp.wait_ge(weights_stored, (LAYERS - 1) * 32)

        @block.tensor
        def _(pe):
            pe.wait_ge(ident_made, 2)
            pe.wait_ge(weights_loaded, LAYERS * 32)
            for l in range(LAYERS):
                for e in range(KD):
                    for q in range(KD):
                        last = nc.tensor.matmul(sum_bank[l][:, e * D:(e + 1) * D],
                                                wt_raw[l][:, KD + q, e * P:(e + 1) * P], wt_raw[l][:, q, :],
                                                start=(q == 0), stop=(q == KD - 1))
                last.then_inc(weight_product, 1)

            with pe.Fori(0, LAYERS) as layer:
                def pair(k, b):
                    if has_pair(k, b, 0):
                        pe.wait_ge(rows_loaded[b], layer * (PAIRS // PAIR_ROUND * 16) + k * 16 + 16)
                        for t in range(2):
                            for e in range(KD):
                                at = (t * KD + e) * P
                                last = nc.tensor.transpose(feature_bank[b % 2][:, at:at + P],
                                                           rows[:, b, t, e * P:(e + 1) * P], ident[:, :])
                        last.then_inc(rows_turned, 1)
                    if not has_pair(k, b, 1):
                        return
                    a = (b - 1) % 2
                    h = pair_features(a)
                    pe.wait_ge(feature_lo, pairs_done(layer, k, b, 1))
                    for t in range(2):
                        for e in range(KD):
                            for i, (w, m) in enumerate(PRODUCTS):
                                last = nc.tensor.matmul(
                                    value_bank[a][:, t * D:(t + 1) * D],
                                    h[:, t, e, w, :], value_weight[:, e, m, :],
                                    start=(e == 0 and i == 0), stop=(e == KD - 1 and i == 2))
                    last.then_inc(value_product, 1)
                    for d in range(KD):
                        for e in range(KD):
                            for i, (w, m) in enumerate(PRODUCTS):
                                last = nc.tensor.matmul(
                                    score_bank[a][:, d * 2 * P:(d + 1) * 2 * P],
                                    score_weight[:, e, w, d * P:(d + 1) * P], h[:, :, e, m, :],
                                    start=(e == 0 and i == 0), stop=(e == KD - 1 and i == 2))
                    last.then_inc(key_product, 1)

                pe.wait_ge(weights_ready, (layer + 1) * 32)
                all_pairs(pe, pair, 1)

                def score(k, c):
                    b = (c // CHUNKS) % 2
                    if c % CHUNKS == 0:
                        pe.wait_ge(query_loaded[b], layer * (16 * PAIRS) + k * 16 + 16)
                    if later(k, c, 0, 4):
                        pe.wait_ge(copied, done(layer, k, c, 4))
                    elif c < 2:
                        pe.wait_ge(key_lo, (layer + 1) * PAIRS - 1 + c)
                    elif c == 2:
                        pe.wait_ge(value_lo, (layer + 1) * PAIRS)
                    col = (c % CHUNKS) * CW
                    for e in range(KD):
                        for i, (a, m) in enumerate(PRODUCTS):
                            last = nc.tensor.matmul(score_bank[c % 4][:, :], query[:, b, e, a, :],
                                                    keys[:, e, m, col:col + CW],
                                                    start=(e == 0 and i == 0), stop=(e == KD - 1 and i == 2))
                    last.then_inc(scored, 1)

                def times_values(k, c):
                    u = (c - LAG_VALUE) % ROUND
                    t = u // CHUNKS
                    first, end = u % CHUNKS == 0, u % CHUNKS == CHUNKS - 1
                    pe.wait_ge(split_lo, done(layer, k, c, LAG_VALUE))
                    if first and later(k, c, LAG_VALUE, ROUND):
                        pe.wait_ge(h_ready, finished_tiles(layer, tile(k, c - LAG_VALUE) - 1))
                    for j in range(BLOCKS):
                        row = (u % CHUNKS) * BLOCKS + j
                        nc.tensor.matmul(sum_bank[t][:, :], split[:, u % 4, j * P:(j + 1) * P],
                                         values[:, row, :, :].rearrange("p s d -> p (s d)"),
                                         start=(first and j == 0), stop=False)
                        last = nc.tensor.matmul(sum_bank[t][:, 0:D],
                                                split[:, u % 4, CW + j * P:CW + (j + 1) * P],
                                                values[:, row, HI, :],
                                                start=False, stop=(end and j == BLOCKS - 1))
                    last.then_inc(summed, 1)

                def step(k, c):
                    if inside(k, c, 0):
                        score(k, c)
                    if inside(k, c, LAG_VALUE):
                        times_values(k, c)
                all_steps(pe, step)

        @block.vector
        def _(dve):
            nc.vector.memset(row_sum[:, :], 0.0).then_inc(h_ready, 1)
            def normalise(i):
                _, first, end = quarter_tiles(i)
                dve.wait_ge(scale_ready, i + 1)
                for t in range(first, end):
                    nc.vector.tensor_scalar(x_all[:, t, :], x_all[:, t, :], rstd[:, t:t + 1], shift[:, t:t + 1],
                                            ALU.mult, ALU.add).then_inc(shifted, 1)
                dve.wait_ge(shifted, sum(DVE_TILES[:i + 1]))
                nc.vector.tensor_scalar(x_all[:, first:end, :], x_all[:, first:end, :], 0.0, None, ALU.max
                                        ).then_inc(normalised[i], end - first)

            for i, g in enumerate(QUARTERS):
                dve.wait_ge(x_loaded[i], 16)
                for t in range(g.start, g.stop):
                    nc.vector.bn_stats(bn[:, t, :], x_all[:, t, :]).then_inc(stats_ready, 1)
                if i > 0:
                    normalise(i - 1)
                dve.wait_ge(var_ready, i + 1)
                nc.vector.reciprocal(rstd[:, g], var[:, g]).then_inc(inv_var_ready, 1)
            for l in range(LAYERS):
                ready, count = (weight_lo, 1) if l else (weights_ready, 16)
                dve.wait_ge(weight_hi, l * 2 + 1)
                nc.vector.tensor_tensor(value_weights[l][:, :, LO, :], wv_raw[l],
                                        value_weights[l][:, :, HI, :].bitcast(F32), ALU.subtract
                                        ).then_inc(ready, count)
                dve.wait_ge(weight_hi, l * 2 + 2)
                nc.vector.tensor_tensor(score_weights[l][:, :, LO, :],
                                        sum_bank[l][:, :].rearrange("p (e d) -> p e d", e=KD),
                                        score_weights[l][:, :, HI, :].bitcast(F32), ALU.subtract
                                        ).then_inc(ready, count)

            normalise(3)

            with dve.Fori(0, LAYERS) as layer:
                def pair(k, b):
                    if has_pair(k, b, 0):
                        h = split[:, 2 + b % 2, :].rearrange("p (t s r) -> p t s r", t=2 * KD, s=2)
                        dve.wait_ge(feature_hi, pairs_done(layer, k, b, 0))
                        nc.vector.tensor_tensor(h[:, :, LO, :],
                                                feature_bank[b % 2][:, :].rearrange("p (t r) -> p t r", r=P),
                                                h[:, :, HI, :].bitcast(F32),
                                                ALU.subtract).then_inc(feature_lo, 1)
                    if has_pair(k, b, 1):
                        a = (b - 1) % 2
                        dve.wait_ge(value_hi, pairs_done(layer, k, b, 1))
                        at = bass.ds(k * (2 * PAIR_ROUND) + 2 * (b - 1), 2)
                        nc.vector.tensor_tensor(values[:, at, LO, :],
                                                value_bank[a][:, :].rearrange("p (t d) -> p t d", t=2),
                                                values[:, at, HI, :].bitcast(F32),
                                                ALU.subtract).then_inc(value_lo, 1)
                        dve.wait_ge(key_hi, pairs_done(layer, k, b, 1))
                        nc.vector.tensor_tensor(pair_keys(LO, k, b - 1), by_run(score_bank[a]),
                                                pair_keys(HI, k, b - 1).bitcast(F32),
                                                ALU.subtract).then_inc(key_lo, 1)

                all_pairs(dve, pair, 1)

                def copy(k, c):
                    t = (c // CHUNKS) % 2
                    dve.wait_ge(scored, done(layer, k, c, 0))
                    if later(k, c, 0, ROUND):
                        dve.wait_ge(shuffled[c // 2 % 2], shuffles_done(layer, k - 1, c))
                    nc.vector.tensor_scalar(scores[:, c, :], score_bank[c % 4][:, :], 1.0, None, ALU.mult,
                                            ALU.max, accum_out=chunk_max[:, t, c % CHUNKS:c % CHUNKS + 1]
                                            ).then_inc(copied, 1)
                    if c % CHUNKS == CHUNKS - 1:
                        dve.wait_ge(copied, done(layer, k, c, 0))
                        nc.vector.tensor_reduce(neg_max[:, t:t + 1], chunk_max[:, t, :], AX.X, ALU.max,
                                                negate=True).then_inc(maxed, 1)

                def turn(k, c):
                    u = (c - LAG_TURN) % ROUND
                    dve.wait_ge(masked, done(layer, k, c, LAG_TURN))
                    nc.vector.transpose(scores[:, u, :], scores[:, u, :]).then_inc(turned, 1)

                def split_turned(k, c):
                    u = (c - LAG_SPLIT) % ROUND
                    dve.wait_ge(split_hi, done(layer, k, c, LAG_SPLIT))
                    nc.vector.tensor_tensor(split[:, u % 4, CW:2 * CW].rearrange("p (j a i) -> p j a i", a=RUNS, i=Q),
                                            turned_chunk(u),
                                            split[:, u % 4, 0:CW].bitcast(F32).rearrange(
                                                "p (j a i) -> p j a i", a=RUNS, i=Q),
                                            ALU.subtract).then_inc(split_lo, 1)

                def invert_sum(k, c, lag):
                    b = ((c - lag) // CHUNKS) % 2
                    T = layer * TILES + tile(k, c - lag)
                    dve.wait_ge(expd, done(layer, k, c, lag - CHUNKS + 1))
                    nc.vector.tensor_reduce(row_sum[:, :], chunk_sum[:, b, :], AX.X, ALU.add
                                            ).then_inc(sum_ready, 1)
                    dve.wait_ge(sum_ready, T + 1)
                    nc.vector.reciprocal(inv_sum[:, :], row_sum[:, :]).then_inc(inv_ready, 1)

                def finish(k, c, lag):
                    b = ((c - lag) // CHUNKS) % 2
                    t = tile(k, c - lag)
                    T = layer * TILES + t
                    dve.wait_ge(low_ready, T + 1)
                    dve.wait_ge(h_stored[b], (layer + 1) * (16 * PAIRS) + k * 16 + 16 * ((c - lag) // ROUND))
                    nc.vector.scalar_tensor_tensor(out=finished[:, b, :], in0=sum_bank[b][:, 0:D],
                                                   scalar=inv_sum[:, :], in1=low_part[:, :],
                                                   op0=ALU.mult, op1=ALU.add).then_inc(finish_step, 1)
                    dve.wait_ge(residual_loaded, (T + 1) * 32)
                    dve.wait_ge(finish_step, T * 3 + 1)
                    nc.vector.tensor_tensor(finished[:, b, :], finished[:, b, :], residual[:, :],
                                            ALU.add).then_inc(finish_step, 1)
                    dve.wait_ge(finish_step, T * 3 + 2)
                    nc.vector.scalar_tensor_tensor(out=finished[:, b, :], in0=finished[:, b, :],
                                                   scalar=SLOPE, in1=finished[:, b, :],
                                                   op0=ALU.mult, op1=ALU.max).then_inc(finish_step, 1)
                    dve.wait_ge(finish_step, T * 3 + 3)
                    nc.vector.tensor_tensor(finished[:, b, :], finished[:, b, :], addend[:, :],
                                            ALU.add).then_inc(h_ready, 1)

                def step(k, c):
                    if inside(k, c, LAG_TURN):
                        turn(k, c)
                    if inside(k, c, LAG_SPLIT):
                        split_turned(k, c)
                    if inside(k, c, 0):
                        copy(k, c)
                    lag = CHUNKS - 1 + LAG_FINISH
                    if (c + 1 - lag) % CHUNKS == 0 and inside(k, c + 1, lag):
                        invert_sum(k, c + 1, lag)
                    if (c - lag) % CHUNKS == 0 and inside(k, c, lag):
                        finish(k, c, lag)
                all_steps(dve, step)

        @block.scalar
        def _(act):
            def root(i):
                act.wait_ge(inv_var_ready, i + 1)
                nc.scalar.activation(rstd[:, QUARTERS[i]], rstd[:, QUARTERS[i]], ACT.Sqrt
                                     ).then_inc(sqrt_ready, 1)

            def normalise(i, first, end):
                for t in range(first, end):
                    nc.scalar.activation(x_all[:, t, :], x_all[:, t, :], ACT.Relu, bias=shift[:, t:t + 1],
                                         scale=rstd[:, t:t + 1]).then_inc(normalised[i], 1)

            root(0)
            act.wait_ge(scale_ready, 1)
            normalise(0, *quarter_tiles(0)[:2])
            root(1)
            act.wait_ge(weights_loaded, LAYERS * 32)
            for l in range(LAYERS):
                nc.scalar.activation(value_weights[l][:, :, HI, :], wv_raw[l], ACT.Copy
                                     ).then_inc(weight_hi, 1)
                act.wait_ge(weight_product, l + 1)
                nc.scalar.activation(score_weights[l][:, :, HI, :],
                                     sum_bank[l][:, :].rearrange("p (e d) -> p e d", e=KD),
                                     ACT.Copy).then_inc(weight_hi, 1)
            for i in (1, 2):
                first, end, _ = quarter_tiles(i)
                act.wait_ge(scale_ready, i + 1)
                normalise(i, first, (first + end) // 2)
                root(i + 1)
                normalise(i, (first + end) // 2, end)
            nc.scalar.preload_act_table(ACT.Exp)
            act.wait_ge(scale_ready, 4)
            normalise(3, *quarter_tiles(3)[:2])

            with act.Fori(0, LAYERS) as layer:
                def pair(k, b):
                    if has_pair(k, b, 0):
                        h = split[:, 2 + b % 2, :].rearrange("p (t s r) -> p t s r", t=2 * KD, s=2)
                        act.wait_ge(rows_turned, pairs_done(layer, k, b, 0))
                        if after(k, b, 0, 2):
                            act.wait_ge(feature_stored[b % 2], layer * (8 * PAIRS) + k * (8 * PAIR_ROUND)
                                        + 16 * (b // 2))
                        nc.scalar.activation(h[:, :, HI, :],
                                             feature_bank[b % 2][:, :].rearrange("p (t r) -> p t r", r=P),
                                             ACT.Copy).then_inc(feature_hi, 1)
                    if has_pair(k, b, 1):
                        a = (b - 1) % 2
                        act.wait_ge(value_product, pairs_done(layer, k, b, 1))
                        nc.scalar.activation(values[:, bass.ds(k * (2 * PAIR_ROUND) + 2 * (b - 1), 2), HI, :],
                                             value_bank[a][:, :].rearrange("p (t d) -> p t d", t=2),
                                             ACT.Copy).then_inc(value_hi, 1)
                        act.wait_ge(key_product, pairs_done(layer, k, b, 1))
                        nc.scalar.activation(pair_keys(HI, k, b - 1), by_run(score_bank[a]), ACT.Copy
                                             ).then_inc(key_hi, 1)

                all_pairs(act, pair, 1)
                act.wait_ge(weights_stored, (LAYERS - 1) * 32)
                for b in range(2):
                    act.wait_ge(feature_stored[b], (layer + 1) * (8 * PAIRS))

                def exponentials(k, c):
                    u = (c - LAG_EXP) % ROUND
                    t = u // CHUNKS
                    if u % CHUNKS == 0:
                        act.wait_ge(maxed, layer * TILES + tile(k, c - LAG_EXP) + 1)
                    nc.scalar.activation(scores[:, u, :], scores[:, u, :], ACT.Exp, bias=neg_max[:, t:t + 1],
                                         accum_out=chunk_sum[:, t, u % CHUNKS:u % CHUNKS + 1]
                                         ).then_inc(expd, 1)

                def split_turned(k, c):
                    u = (c - LAG_SPLIT) % ROUND
                    if u % 2 == 0:
                        act.wait_ge(shuffled[u // 2 % 2], shuffles_done(layer, k + (c - LAG_SPLIT) // ROUND, u))
                    if later(k, c, LAG_SPLIT, 3):
                        act.wait_ge(summed, done(layer, k, c, LAG_SPLIT + 3))
                    nc.scalar.activation(split[:, u % 4, 0:CW].rearrange("p (j a i) -> p j a i", a=RUNS, i=Q),
                                         turned_chunk(u), ACT.Copy).then_inc(split_hi, 1)

                def scale_low(k, c, lag):
                    b = ((c - lag) // CHUNKS) % 2
                    T = layer * TILES + tile(k, c - lag)
                    act.wait_ge(summed, done(layer, k, c, LAG_FINISH))
                    act.wait_ge(inv_ready, T + 1)
                    nc.scalar.activation(low_part[:, :], sum_bank[b][:, D:2 * D], ACT.Copy,
                                         scale=inv_sum[:, :]).then_inc(low_ready, 1)

                def store(k, c, lag):
                    b = ((c - lag) // CHUNKS) % 2
                    t = tile(k, c - lag)
                    act.wait_ge(h_ready, finished_tiles(layer, t + 1))
                    act.dma_start(out_tiles[bass.ds(t, 1), :, :].rearrange("o p d -> p (o d)"),
                                  finished[:, b, :]).then_inc(h_stored[b], 16)

                def step(k, c):
                    if inside(k, c, LAG_EXP):
                        exponentials(k, c)
                    if inside(k, c, LAG_SPLIT):
                        split_turned(k, c)
                    lag = CHUNKS - 1 + LAG_FINISH
                    if (c - lag) % CHUNKS == 0 and inside(k, c, lag):
                        scale_low(k, c, lag)
                    lag += 1
                    last = isinstance(k, int) and tile(k, c - lag) == TILES - 1
                    if (c - lag) % CHUNKS == 0 and inside(k, c, lag) and not last:
                        store(k, c, lag)
                all_steps(act, step)

        @block.gpsimd
        def _(pool):
            nc.gpsimd.memset(ident[:, :], 0.0).then_inc(ident_made, 1)
            pool.wait_ge(ident_made, 1)
            nc.gpsimd.affine_select(out=ident[:, :], in_=ident[:, :], compare_op=ALU.not_equal, fill=1.0,
                                    base=0, pattern=[[-1, P]], channel_multiplier=1).then_inc(ident_made, 1)

            n = [0]

            def link(instruction):
                n[0] += 1
                instruction.then_inc(norm_step, 1)
                pool.wait_ge(norm_step, n[0])

            def scalar(out, in_, factor, term=0.0):
                return nc.gpsimd.tensor_scalar(out, in_, factor, term, ALU.mult, ALU.add)

            for i, g in enumerate(QUARTERS):
                pool.wait_ge(stats_ready, (i + 1) * (TILES // 4))
                link(nc.gpsimd.tensor_tensor(tmp[:, g], bn[:, g, 1], bn[:, g, 4], ALU.subtract))
                link(nc.gpsimd.tensor_tensor(tmp[:, g], tmp[:, g], tmp[:, g], ALU.mult))
                link(scalar(tmp[:, g], tmp[:, g], 0.25, EPS))
                link(nc.gpsimd.tensor_tensor(var[:, g], bn[:, g, 2], bn[:, g, 5], ALU.add))
                link(scalar(var[:, g], var[:, g], 1.0 / D))
                nc.gpsimd.tensor_tensor(var[:, g], var[:, g], tmp[:, g], ALU.add).then_inc(var_ready, 1)
                link(nc.gpsimd.tensor_tensor(mean[:, g], bn[:, g, 1], bn[:, g, 4], ALU.add))
                link(scalar(mean[:, g], mean[:, g], -0.5))
                pool.wait_ge(sqrt_ready, i + 1)
                link(nc.gpsimd.tensor_tensor(tmp[:, g], rstd[:, g], rstd[:, g], ALU.mult))
                link(nc.gpsimd.tensor_tensor(tmp[:, g], tmp[:, g], var[:, g], ALU.mult))
                link(scalar(tmp[:, g], tmp[:, g], -0.5, 1.5))
                link(nc.gpsimd.tensor_tensor(rstd[:, g], rstd[:, g], tmp[:, g], ALU.mult))
                nc.gpsimd.tensor_tensor(shift[:, g], mean[:, g], rstd[:, g], ALU.mult).then_inc(scale_ready, 1)
                if POOL_TILES[i]:
                    pool.wait_ge(scale_ready, i + 1)
                for t in range(quarter_tiles(i)[2], g.stop):
                    link(nc.gpsimd.tensor_scalar(x_all[:, t, :], x_all[:, t, :], rstd[:, t:t + 1],
                                                 shift[:, t:t + 1], ALU.mult, ALU.add))
                    nc.gpsimd.tensor_scalar(x_all[:, t, :], x_all[:, t, :], 0.0, None, ALU.max
                                            ).then_inc(normalised[i], 1)

            with pool.Fori(0, LAYERS) as layer:
                def step(k, c):
                    if not inside(k, c, LAG_EXP):
                        return
                    u = (c - LAG_EXP) % ROUND
                    slot = (u // 2) % ADJ_SLOTS
                    pool.wait_ge(expd, done(layer, k, c, LAG_EXP))
                    if u % 2 == 0:
                        pool.wait_ge(adj_loaded[slot], layer * (32 * ROUNDS) + k * 32
                                     + 16 * ((c - LAG_EXP) // (2 * ADJ_SLOTS) + 1))
                    half = (u % 2) * CW
                    nc.gpsimd.tensor_tensor(scores[:, u, :], scores[:, u, :],
                                            adj_ring[:, slot, half:half + CW], ALU.mult).then_inc(masked, 1)

                all_steps(pool, step)


def kernel(x, adj, L0_gnn_W_stack):
    import numpy as np
    import concourse.bacc as bacc
    from concourse.bass_utils import run_bass_kernel_spmd

    x, adj, w = (np.asarray(a) for a in (x, adj, L0_gnn_W_stack))
    n, d = x.shape
    group, run_tiles, quarters = 1024, 8, 4
    arrays = {
        "x_padded": np.ascontiguousarray(np.concatenate([np.zeros((P, d), x.dtype), x])),
        "adj": np.ascontiguousarray(
            adj.reshape(n, n // group, run_tiles, P // quarters, quarters).transpose(0, 1, 4, 2, 3)
            .reshape(n, n)),
        "w_value": np.ascontiguousarray(w[:, :, 0:d]),
        "w_transposed": np.ascontiguousarray(w.transpose(0, 2, 1)),
    }
    nc = bacc.Bacc("TRN2", target_bir_lowering=False, num_devices=1, dynamic_dma_scratch_size=1024)
    ins = [nc.dram_tensor(n, a.shape, mybir.dt.from_np(a.dtype), kind="ExternalInput").ap()
           for n, a in arrays.items()]
    out = nc.dram_tensor("out", x.shape, mybir.dt.from_np(x.dtype), kind="ExternalOutput").ap()
    gnn_kernel(nc, *ins, out)
    result = run_bass_kernel_spmd(nc, [arrays], core_ids=[0])
    return result.results[0]["out"]
```
